# Optimizing a Trainium2 kernel written in Bass

```python
import numpy as np
import jax
import jax.numpy as jnp

def _softmax(x, axis=-1):
    return jax.nn.softmax(x, axis=axis)

def _gelu(x):
    return jax.nn.gelu(x, approximate=True)

def _silu(x):
    return jax.nn.silu(x)

def _sigmoid(x):
    return jax.nn.sigmoid(x)

def _layernorm(x, axis=-1, eps=1e-05):
    m = jnp.mean(x, axis=axis, keepdims=True)
    v = jnp.var(x, axis=axis, keepdims=True)
    return (x - m) / jnp.sqrt(v + eps)

def _scatter_add(tgt, idx, src, axis=0):
    return tgt.at[idx].add(src)

def _segment_sum(src, seg, n):
    return jax.ops.segment_sum(src, seg, n)
kernel_name = 'mk_gnn_resnorm_d1_gnn_r8_38a1e5'

def setup_inputs(seed: int=0):
    np.random.seed(seed)
    _w = jnp.asarray

    def _rec_inputs():
        import jax
        import jax.numpy as jnp
        _gk = jax.random.key(seed)
        x = -0.0005121 + 1.001 * jax.random.normal(jax.random.fold_in(_gk, 1), (12500, 64), jnp.float32)
        src = jax.random.randint(jax.random.fold_in(_gk, 2), (400000,), 0, 12500, jnp.int32)
        dst = jnp.minimum((12500 * jax.random.uniform(jax.random.fold_in(_gk, 3), (400000,)) ** 2.0).astype(jnp.int32), 99999)
        _o = jnp.argsort(dst, stable=True)
        src = src[_o]
        dst = dst[_o]
        edge_attr_64 = -8.16379e-05 + 0.999858 * jax.random.normal(jax.random.fold_in(_gk, 12), (400000, 64), jnp.float32)
        return (x, src, dst, edge_attr_64)
    x, src, dst, edge_attr_64 = _rec_inputs()

    def _L0_gnn_setup():
        import jax, jax.numpy as jnp
        import numpy as np
        BN_EPS = 1e-05

        def _batchnorm(x, gamma, beta):
            mean = jnp.mean(x, axis=0)
            var = jnp.mean(jnp.square(x - mean), axis=0)
            return (x - mean) * jax.lax.rsqrt(var + BN_EPS) * gamma + beta
        key = jax.random.key(seed)
        ks = jax.random.split(key, 6)
        N, E, D_atom, D_nbr = (6250, 200000, 64, 64)
        d_in, d_out = (2 * D_atom + D_nbr, 2 * D_atom)
        return {'atom_in_fea': jax.random.normal(ks[0], (N, D_atom), dtype=jnp.float32), 'nbr_fea': jax.random.normal(ks[1], (E, D_nbr), dtype=jnp.float32), 'edge_src': jax.random.randint(ks[2], (E,), 0, N), 'edge_dst': jax.random.randint(ks[3], (E,), 0, N), 'W': jax.random.normal(ks[4], (d_in, d_out), dtype=jnp.float32) * (1.0 / np.sqrt(d_in)), 'b': jax.random.normal(ks[5], (d_out,), dtype=jnp.float32) * 0.01, 'bn1_gamma': jnp.ones((d_out,), dtype=jnp.float32), 'bn1_beta': jnp.zeros((d_out,), dtype=jnp.float32), 'bn2_gamma': jnp.ones((D_atom,), dtype=jnp.float32), 'bn2_beta': jnp.zeros((D_atom,), dtype=jnp.float32)}
    _L0_gnn_all = _L0_gnn_setup()
    _L0_gnn_in = {k: v for k, v in _L0_gnn_all.items() if k in ('W', 'b', 'bn1_gamma', 'bn1_beta', 'bn2_gamma', 'bn2_beta')}
    del _L0_gnn_all
    return {'x': x, 'src': src, 'dst': dst, 'edge_attr_64': edge_attr_64, 'L0_gnn_W': _L0_gnn_in['W'], 'L0_gnn_b': _L0_gnn_in['b'], 'L0_gnn_bn1_gamma': _L0_gnn_in['bn1_gamma'], 'L0_gnn_bn1_beta': _L0_gnn_in['bn1_beta'], 'L0_gnn_bn2_gamma': _L0_gnn_in['bn2_gamma'], 'L0_gnn_bn2_beta': _L0_gnn_in['bn2_beta']}

def reference(x, src, dst, edge_attr_64, L0_gnn_W, L0_gnn_b, L0_gnn_bn1_gamma, L0_gnn_bn1_beta, L0_gnn_bn2_gamma, L0_gnn_bn2_beta):
    import jax
    import jax.numpy as jnp

    def _L0_gnn_ref(atom_in_fea, nbr_fea, edge_src, edge_dst, W, b, bn1_gamma, bn1_beta, bn2_gamma, bn2_beta):
        import jax, jax.numpy as jnp
        import numpy as np
        BN_EPS = 1e-05

        def _batchnorm(x, gamma, beta):
            mean = jnp.mean(x, axis=0)
            var = jnp.mean(jnp.square(x - mean), axis=0)
            return (x - mean) * jax.lax.rsqrt(var + BN_EPS) * gamma + beta
        N, D = atom_in_fea.shape
        total_fea = jnp.concatenate([atom_in_fea[edge_src], atom_in_fea[edge_dst], nbr_fea], axis=1)
        total_fea = _batchnorm(total_fea @ W + b, bn1_gamma, bn1_beta)
        filter_fea, core_fea = jnp.split(total_fea, 2, axis=1)
        nbr_msg = jax.nn.sigmoid(filter_fea) * jax.nn.softplus(core_fea)
        atom_update = jax.ops.segment_sum(nbr_msg, edge_dst, num_segments=N)
        atom_update = _batchnorm(atom_update, bn2_gamma, bn2_beta)
        return jax.nn.softplus(atom_in_fea + atom_update)
    x = _layernorm(x + _L0_gnn_ref(x, edge_attr_64, src, dst, L0_gnn_W, L0_gnn_b, L0_gnn_bn1_gamma, L0_gnn_bn1_beta, L0_gnn_bn2_gamma, L0_gnn_bn2_beta), axis=-1)
    return x

_drawn_inputs = setup_inputs


def setup_inputs(seed=0):
    import zlib

    import numpy as np

    out = dict(_drawn_inputs(seed))
    spreads = {'L0_gnn_bn1_gamma': (1.0, 0.6),
     'L0_gnn_bn1_beta': (0.0, 2.0),
     'L0_gnn_bn2_gamma': (1.0, 0.2),
     'L0_gnn_bn2_beta': (0.0, 0.1)}
    factors = {'edge_attr_64': 2.749, 'L0_gnn_b': 64.0}
    for name, (base, spread) in spreads.items():
        noise = np.random.default_rng([zlib.crc32(name.encode()), seed]).standard_normal(out[name].shape)
        drawn = base * np.exp(spread * noise) if base else spread * noise
        out[name] = jnp.asarray(drawn.astype(out[name].dtype))
    for name, factor in factors.items():
        out[name] = (out[name] * factor).astype(out[name].dtype)
    return out
```

```python
from contextlib import ExitStack

import numpy as np

import concourse.bass as bass
from concourse import mybir

F32 = mybir.dt.float32
BF16 = mybir.dt.bfloat16
I32 = mybir.dt.int32
ALU = mybir.AluOpType
ACT = mybir.ActivationFunctionType
AX_X = mybir.AxisListType.X

P = 128
D = 64
Z = 2 * D
TILE = 128
TPC = 5
CH = TPC * TILE
HALF = CH // 2
BANK = 512
SLOTS = 5
STEP = 64
PARTS = 3
GROUP = 4
PPH = 4
EPS = 1e-5
SP_CAP = 30.0


def sizes(n_nodes, n_edges):
    chunks = n_edges // CH
    assert chunks * CH == n_edges and chunks % SLOTS == 0
    blocks = -(-n_nodes // P)
    windows = (n_nodes - 1) // STEP + 1
    groups = -(-((windows - 1) * STEP + P) // (GROUP * P))
    groups += groups % 2
    pairs = -(-chunks // 2)
    return chunks, blocks, windows, groups, pairs


def build_program(nc, a, out):
    n_nodes = a["x"].shape[0]
    n_edges = a["src_cols"].shape[1] * TILE
    chunks, blocks, windows, groups, pairs = sizes(n_nodes, n_edges)
    tiles = chunks * TPC
    pair_tiles = 2 * pairs * TPC
    steps = chunks // SLOTS
    last_rows = n_nodes - (blocks - 1) * P
    max_row = (windows - 1) * STEP
    all_windows = blocks
    idx_groups = -(-chunks // P)
    assert chunks % idx_groups == 0 and 2 * blocks <= windows + 1
    per_group = chunks // idx_groups

    table = nc.dram_tensor("dst_table", (groups * GROUP * P, PARTS * Z), BF16, kind="Internal").ap()
    z_gate = nc.dram_tensor("z_gate", (2 * pairs * D, CH), F32, kind="Internal").ap()
    z_core = nc.dram_tensor("z_core", (2 * pairs * D, CH), F32, kind="Internal").ap()

    keep = ExitStack()
    with keep:
        def sb_in(ctx, name, shape, dt=F32):
            return ctx.enter_context(nc.sbuf_tensor(name, shape, dt))

        def sem(name):
            return keep.enter_context(nc.semaphore(name))

        ident = sb_in(keep, "ident", [P, P])
        iota_row = sb_in(keep, "iota_row", [P, P])
        dst_f = sb_in(keep, "dst_f", [P, pair_tiles])
        dst_local = sb_in(keep, "dst_local", [P, pair_tiles])
        base_i = sb_in(keep, "base_i", [P, 2 * pairs], I32)
        unfit = sb_in(keep, "unfit", [1, 1], I32)
        affine = sb_in(keep, "affine", [P, 2])

        pass1(nc, a, sem, keep, sb_in, locals())
        sums = sb_in(keep, "sums", [P, 2 * blocks * D])
        pass2(nc, a, sem, keep, sb_in, locals())
        nodes(nc, a, out, sem, keep, sb_in, locals())
    return nc


def pass1(nc, a, sem, keep, sb_in, g):
    chunks, groups, pairs, tiles, steps = g["chunks"], g["groups"], g["pairs"], g["tiles"], g["steps"]
    pair_tiles, max_row, idx_groups, per_group = g["pair_tiles"], g["max_row"], g["idx_groups"], g["per_group"]
    table, z_gate, z_core = g["table"], g["z_gate"], g["z_core"]
    ident, iota_row, dst_f, dst_local, base_i = g["ident"], g["iota_row"], g["dst_f"], g["dst_local"], g["base_i"]
    unfit, affine = g["unfit"], g["affine"]
    halves = 2 * chunks

    ctx = ExitStack()
    with ctx:
        def sb(name, shape, dt=F32):
            return sb_in(ctx, name, shape, dt)

        def ps(name, shape):
            return ctx.enter_context(nc.psum_tensor(name, shape, F32))

        ident_bf = sb("ident_bf", [P, P], BF16)
        iota_col = sb("iota_col", [P, 1])
        w_both = sb("w_both", [P, Z])
        w_dst = sb("w_dst", [D, Z])
        bias = sb("bias", [P, 1])
        bn1 = sb("bn1", [P, 2])
        src_all = sb("src_all", [P, tiles + SLOTS * TPC], I32)
        dst_i = sb("dst_i", [P, tiles], I32)
        dst_bf = sb("dst_bf", [P, tiles], BF16)
        least = sb("least", [P, chunks])
        least_t = sb("least_t", [P, idx_groups])
        base_f = sb("base_f", [P, chunks])
        top = sb("top", [P, 1])
        top_one = sb("top_one", [1, 4])
        x_group = sb("x_group", [D, 2, GROUP * P])
        rest = sb("rest", [P, 2, GROUP * Z])
        parts = sb("parts", [P, 2, GROUP, PARTS, Z], BF16)
        src_idx = sb("src_idx", [P, SLOTS, TPC], I32)
        dst_idx = sb("dst_idx", [P, TPC], I32)
        x_src = sb("x_src", [P, SLOTS, TPC * D])
        x_dst = sb("x_dst", [P, TPC * D])
        feats = sb("feats", [P, SLOTS, CH])
        x_dst_t = sb("x_dst_t", [D, CH])
        window = sb("window", [P, SLOTS, PARTS * Z], BF16)
        onehot_t = sb("onehot_t", [P, SLOTS, CH], BF16)
        z_out = sb("z_out", [P, SLOTS, CH])
        stats = sb("stats", [P, 6 * halves])
        moments = sb("moments", [P, 2])
        small = sb("small", [P, 4])
        zero = sb("zero", [D, CH])

        xt_ps = ps("xt_ps", [P, 2 * BANK])
        dst_ps = ps("dst_ps", [P, 2 * BANK])
        z_ps = ps("z_ps", [P, 2 * BANK])
        pre_ps = ps("pre_ps", [P, 2, BANK])
        z_halves = z_ps[:, :].rearrange("p (h n) -> p h n", n=BANK)[:, :, 0:HALF]

        consts_loaded = sem("consts_loaded")
        src_loaded = sem("src_loaded")
        dst_loaded = sem("dst_loaded")
        zero_made = sem("zero_made")
        pad_stored = sem("pad_stored")
        x_group_loaded = [sem(f"x_group_loaded{k}") for k in range(2)]
        window_step = sem("window_step")
        least_moved = sem("least_moved")
        least_spread = sem("least_spread")
        top_moved = sem("top_moved")
        unfit_known = sem("unfit_known")
        table_product = sem("table_product")
        part_hi = sem("part_hi")
        part_rest = sem("part_rest")
        part_mid = sem("part_mid")
        part_lo = sem("part_lo")
        table_stored = [sem(f"table_stored{k}") for k in range(2)]
        ident_cast = sem("ident_cast")
        idx_copied = sem("idx_copied")
        src_gathered = [sem(f"src_gathered{j}") for j in range(SLOTS)]
        gathers_due = sem("gathers_due")
        turns_due = sem("turns_due")
        dst_spread = sem("dst_spread")
        onehot_done = sem("onehot_done")
        xt_done = sem("xt_done")
        xt_copied = sem("xt_copied")
        edges_loaded = [sem(f"edges_loaded{j}") for j in range(SLOTS)]
        window_loaded = [sem(f"window_loaded{j}") for j in range(SLOTS)]
        z_done = sem("z_done")
        z_copied = sem("z_copied")
        stats_done = sem("stats_done")
        z_stored = [sem(f"z_stored{j}") for j in range(SLOTS)]
        affine_step = sem("affine_step")
        any_idx = sem("any_idx")
        any_gathered = sem("any_gathered")
        any_turned = sem("any_turned")
        any_src_copied = sem("any_src_copied")
        any_dst_copied = sem("any_dst_copied")
        any_edges = sem("any_edges")
        any_z = sem("any_z")
        any_z_copied = sem("any_z_copied")
        any_stats = sem("any_stats")
        any_stored = sem("any_stored")

        block = ctx.enter_context(nc.Block())
        N_CONSTS = 9

        def flag(eng):
            return eng.value_load(unfit[0:1, 0:1], min_val=0, max_val=1)

        @block.sync
        def _(sp):
            sp.dma_start(dst_i[:, :], a["dst_cols"]).then_inc(dst_loaded, 16)
            sp.dma_start(ident[:, :], a["ident"]).then_inc(consts_loaded, 16)
            sp.dma_start(iota_row[:, :], a["iota_row"]).then_inc(consts_loaded, 16)
            sp.dma_start(iota_col[:, :], a["iota_col"]).then_inc(consts_loaded, 16)
            sp.dma_start(w_both[0:D, :], a["w"][0:D, :]).then_inc(consts_loaded, 16)
            sp.dma_start(w_both[D:P, :], a["w"][2 * D:3 * D, :]).then_inc(consts_loaded, 16)
            sp.dma_start(w_dst[:, :], a["w"][D:2 * D, :]).then_inc(consts_loaded, 16)
            sp.dma_start(bias[:, :], a["b"]).then_inc(consts_loaded, 16)
            sp.dma_start(bn1[:, 0:1], a["gamma1"]).then_inc(consts_loaded, 16)
            sp.dma_start(bn1[:, 1:2], a["beta1"]).then_inc(consts_loaded, 16)
            sp.dma_start(src_all[:, 0:tiles], a["src_cols"]).then_inc(src_loaded, 16)
            for k in range(2):
                sp.dma_start(x_group[:, k, :], a["x_groups"][k * D:(k + 1) * D, :]).then_inc(x_group_loaded[k], 16)
            with sp.Fori(1, groups // 2) as i:
                for k in range(2):
                    sp.wait_ge(table_product, 2 * i + k - 1)
                    sp.dma_start(x_group[:, k, :], a["x_groups"][bass.ds((2 * i + k) * D, D), :])\
                        .then_inc(x_group_loaded[k], 16)
            if 2 * pairs > chunks:
                sp.wait_ge(zero_made, 1)
                sp.dma_start(z_gate[chunks * D:, :], zero[:, :]).then_inc(pad_stored, 16)
                sp.dma_start(z_core[chunks * D:, :], zero[:, :]).then_inc(pad_stored, 16)
            for k in range(2):
                sp.wait_ge(table_stored[k], 16 * (groups // 2))
            sp.wait_ge(unfit_known, 1)

            def load_chunk(i, j, first):
                c = i * SLOTS + j
                if not first:
                    sp.wait_ge(z_done, c - SLOTS + 1)
                sp.dma_start(feats[D:P, j, :], a["edge_chunks"][bass.ds(c * D, D), :]).then_inc(edges_loaded[j], 16)
                row = sp.value_load(base_i[0:1, bass.ds(c, 1)], min_val=0, max_val=max_row)
                sp.dma_start(window[:, j, :], table[bass.ds(row, P), :]).then_inc(window_loaded[j], 16)

            with sp.If(flag(sp) < 1):
                for j in range(SLOTS):
                    load_chunk(0, j, True)
                with sp.Fori(1, steps) as i:
                    for j in range(SLOTS):
                        load_chunk(i, j, False)
            with sp.Else():
                with sp.Fori(0, chunks) as c:
                    sp.wait_ge(any_idx, c + 1)
                    sp.dma_start(feats[D:P, 0, :], a["edge_chunks"][bass.ds(c * D, D), :]).then_inc(any_edges, 16)
                    sp.wait_ge(any_z_copied, c + 1)
                    sp.dma_start(z_gate[bass.ds(c * D, D), :], z_out[0:D, 0, :]).then_inc(any_stored, 16)
                    sp.dma_start(z_core[bass.ds(c * D, D), :], z_out[D:P, 0, :]).then_inc(any_stored, 16)
                sp.wait_ge(any_stored, 32 * chunks)
            if 2 * pairs > chunks:
                sp.wait_ge(pad_stored, 32)

        @block.gpsimd
        def _(pool):
            nc.gpsimd.memset(zero[:, :], 0.0).then_inc(zero_made, 1)
            pool.wait_ge(unfit_known, 1)

            def gather(rows, idx, done):
                pool.sem_inc(gathers_due, 1)
                for t in range(TPC):
                    pool.indirect_dma_start(
                        rows[:, t * D:(t + 1) * D], None, a["x"],
                        bass.IndirectOffsetOnAxis(ap=idx[:, t:t + 1], axis=0)).then_inc(done, 16)

            def gather_chunk(i, j, first):
                c = i * SLOTS + j
                pool.wait_ge(idx_copied, c + 1)
                if not first:
                    pool.wait_ge(xt_done, c - SLOTS + 1)
                gather(x_src[:, j, :], src_idx[:, j, :], src_gathered[j])

            with pool.If(flag(pool) < 1):
                for j in range(SLOTS):
                    gather_chunk(0, j, True)
                with pool.Fori(1, steps) as i:
                    for j in range(SLOTS):
                        gather_chunk(i, j, False)
            with pool.Else():
                with pool.Fori(0, chunks) as c:
                    pool.wait_ge(any_idx, c + 1)
                    gather(x_src[:, 0, :], src_idx[:, 0, :], any_gathered)
                    gather(x_dst[:, :], dst_idx[:, :], any_gathered)
            pool.wait_ge(affine_step, 3)
            nc.gpsimd.tensor_tensor(small[:, 2:3], small[:, 0:1], small[:, 1:2], ALU.pow).then_inc(affine_step, 1)

        @block.vector
        def _(dve):
            done = [0]

            def step(ins):
                done[0] += 1
                ins.then_inc(window_step, 1)
                dve.wait_ge(window_step, done[0])

            step(nc.vector.memset(dst_f[:, :], -1.0))
            step(nc.vector.memset(dst_local[:, :], -1.0))
            step(nc.vector.memset(base_i[:, :], 0))
            step(nc.vector.memset(src_all[:, tiles:], 0))
            dve.wait_ge(consts_loaded, 16 * N_CONSTS)
            nc.vector.tensor_copy(ident_bf[:, :], ident[:, :]).then_inc(ident_cast, 1)
            dve.wait_ge(dst_loaded, 16)
            step(nc.vector.tensor_copy(dst_f[:, 0:tiles], dst_i[:, :]))
            step(nc.vector.tensor_reduce(
                least[:, :], dst_f[:, 0:tiles].rearrange("p (c t) -> p c t", t=TPC), AX_X, ALU.min))
            dve.wait_ge(least_moved, 1)
            step(nc.vector.tensor_reduce(
                least_t[0:per_group, :],
                xt_ps[0:per_group, 0:idx_groups * P].rearrange("p (g k) -> p g k", k=P), AX_X, ALU.min))
            dve.wait_ge(least_spread, 1)
            step(nc.vector.tensor_copy(
                base_i[:, 0:chunks].rearrange("p (g k) -> p g k", k=per_group),
                dst_ps[:, 0:idx_groups * P].rearrange("p (g k) -> p g k", k=P)[:, :, 0:per_group]))
            shift = STEP.bit_length() - 1
            step(nc.vector.tensor_scalar(base_i[:, 0:chunks], base_i[:, 0:chunks], shift, shift,
                                         ALU.logical_shift_right, ALU.logical_shift_left))
            step(nc.vector.tensor_copy(base_f[:, :], base_i[:, 0:chunks]))
            step(nc.vector.tensor_tensor(
                dst_local[:, 0:tiles].rearrange("p (c t) -> p c t", t=TPC),
                dst_f[:, 0:tiles].rearrange("p (c t) -> p c t", t=TPC),
                base_f[:, :].unsqueeze(2).broadcast_to([P, chunks, TPC]), ALU.subtract))
            step(nc.vector.tensor_reduce(top[:, :], dst_local[:, 0:tiles], AX_X, ALU.max))
            dve.wait_ge(top_moved, 1)
            step(nc.vector.tensor_reduce(top_one[:, 0:1], xt_ps[0:1, 0:P], AX_X, ALU.max))
            step(nc.vector.tensor_scalar(top_one[:, 1:2], top_one[:, 0:1], float(P), None, ALU.is_ge))
            nc.vector.tensor_copy(unfit[:, :], top_one[:, 1:2]).then_inc(unfit_known, 1)
            step(nc.vector.tensor_copy(dst_bf[:, :], dst_local[:, 0:tiles]))
            dve.wait_ge(src_loaded, 16)
            for j in range(SLOTS):
                nc.vector.tensor_copy(src_idx[:, j, :], src_all[:, j * TPC:(j + 1) * TPC]).then_inc(idx_copied, 1)
            dve.wait_ge(unfit_known, 1)

            def table_group(i, k, first):
                n = 2 * i + k
                dve.wait_ge(part_hi, n + 1)
                hi = parts[:, k, :, 0, :]
                mid = parts[:, k, :, 1, :]
                rest_k = rest[:, k, :].rearrange("p (b z) -> p b z", z=Z)
                if not first:
                    dve.wait_ge(part_lo, n - 1)
                nc.vector.tensor_tensor(rest_k, pre_ps[:, k, :].rearrange("p (b z) -> p b z", z=Z), hi,
                                        ALU.subtract).then_inc(part_rest, 1)
                dve.wait_ge(part_mid, n + 1)
                nc.vector.tensor_tensor(parts[:, k, :, 2, :], rest_k, mid, ALU.subtract).then_inc(part_lo, 1)

            for k in range(2):
                table_group(0, k, True)
            with dve.Fori(1, groups // 2) as i:
                for k in range(2):
                    table_group(i, k, False)

            def chunk(i, j, first):
                c = i * SLOTS + j
                dve.wait_ge(dst_spread, c + 1)
                if not first:
                    dve.wait_ge(z_done, c - SLOTS + 1)
                nc.vector.tensor_scalar(onehot_t[:, j, :], dst_ps[:, 0:CH], iota_col[:, 0:1], None,
                                        ALU.is_equal).then_inc(onehot_done, 1)
                dve.wait_ge(xt_done, c + 1)
                nc.vector.tensor_copy(src_idx[:, j, :], src_all[:, bass.ds((c + SLOTS) * TPC, TPC)])\
                    .then_inc(idx_copied, 1)
                dve.wait_ge(z_copied, c + 1)
                for h in range(2):
                    last = nc.vector.bn_stats(stats[:, bass.ds((2 * c + h) * 6, 6)],
                                              z_out[:, j, h * HALF:(h + 1) * HALF])
                last.then_inc(stats_done, 1)

            with dve.If(flag(dve) < 1):
                for j in range(SLOTS):
                    chunk(0, j, True)
                with dve.Fori(1, steps) as i:
                    for j in range(SLOTS):
                        chunk(i, j, False)
                dve.wait_ge(stats_done, chunks)
            with dve.Else():
                def any_chunk(c, first):
                    if not first:
                        dve.wait_ge(any_stats, c)
                    nc.vector.tensor_copy(src_idx[:, 0, :], src_all[:, bass.ds(c * TPC, TPC)])\
                        .then_inc(window_step, 1)
                    dve.wait_ge(window_step, done[0] + 1 + c)
                    nc.vector.tensor_copy(dst_idx[:, :], dst_i[:, bass.ds(c * TPC, TPC)]).then_inc(any_idx, 1)
                    dve.wait_ge(any_turned, c + 1)
                    nc.vector.tensor_copy(x_dst_t[:, :], dst_ps[0:D, 0:CH]).then_inc(any_dst_copied, 1)
                    dve.wait_ge(any_z_copied, c + 1)
                    for h in range(2):
                        last = nc.vector.bn_stats(stats[:, bass.ds((2 * c + h) * 6, 6)],
                                                  z_out[:, 0, h * HALF:(h + 1) * HALF])
                    last.then_inc(any_stats, 1)

                any_chunk(0, True)
                with dve.Fori(1, chunks) as c:
                    any_chunk(c, False)
                dve.wait_ge(any_stats, chunks)

            nc.vector.bn_aggr(moments[:, :], stats[:, :]).then_inc(affine_step, 1)
            dve.wait_ge(affine_step, 1)
            nc.vector.tensor_scalar(small[:, 0:1], moments[:, 1:2], EPS, None, ALU.add).then_inc(affine_step, 1)
            nc.vector.memset(small[:, 1:2], -0.5).then_inc(affine_step, 1)
            dve.wait_ge(affine_step, 4)
            nc.vector.tensor_tensor(affine[:, 0:1], small[:, 2:3], bn1[:, 0:1], ALU.mult).then_inc(affine_step, 1)
            dve.wait_ge(affine_step, 5)
            nc.vector.tensor_tensor(small[:, 3:4], moments[:, 0:1], affine[:, 0:1], ALU.mult).then_inc(affine_step, 1)
            dve.wait_ge(affine_step, 6)
            nc.vector.tensor_tensor(affine[:, 1:2], bn1[:, 1:2], small[:, 3:4], ALU.subtract).then_inc(affine_step, 1)
            dve.wait_ge(affine_step, 7)

        @block.tensor
        def _(pe):
            pe.wait_ge(consts_loaded, 16 * N_CONSTS)
            pe.wait_ge(window_step, 6)
            for k in range(idx_groups):
                last = nc.tensor.transpose(xt_ps[0:per_group, k * P:(k + 1) * P],
                                           least[:, k * per_group:(k + 1) * per_group], ident[:, :])
            last.then_inc(least_moved, 1)
            pe.wait_ge(window_step, 7)
            for k in range(idx_groups):
                last = nc.tensor.matmul(dst_ps[:, k * P:k * P + per_group],
                                        least_t[0:per_group, k:k + 1].broadcast_to([per_group, P]),
                                        ident[0:per_group, 0:per_group], start=True, stop=True)
            last.then_inc(least_spread, 1)
            pe.wait_ge(window_step, 12)
            nc.tensor.transpose(xt_ps[0:1, 0:P], top[:, 0:1], ident[:, :]).then_inc(top_moved, 1)

            def table_group(i, k, first):
                n = 2 * i + k
                pe.wait_ge(x_group_loaded[k], 16 * (i + 1))
                if not first:
                    pe.wait_ge(part_rest, n - 1)
                for m in range(GROUP):
                    last = nc.tensor.matmul(pre_ps[:, k, m * Z:(m + 1) * Z], x_group[:, k, m * P:(m + 1) * P],
                                            w_dst[:, :], start=True, stop=True)
                last.then_inc(table_product, 1)

            for k in range(2):
                table_group(0, k, True)
            with pe.Fori(1, groups // 2) as i:
                for k in range(2):
                    table_group(i, k, False)
            pe.wait_ge(unfit_known, 1)
            pe.wait_ge(ident_cast, 1)
            pe.wait_ge(window_step, 15)

            def turn(to, rows):
                pe.sem_inc(turns_due, 1)
                for t in range(TPC):
                    last = nc.tensor.transpose(to[0:D, t * TILE:(t + 1) * TILE], rows[:, t * D:(t + 1) * D],
                                               ident[:, :])
                return last

            def chunk(i, j, first):
                c = i * SLOTS + j
                if not (first and j == 0):
                    pe.wait_ge(onehot_done, c)
                for t in range(TPC):
                    last = nc.tensor.matmul(dst_ps[:, t * TILE:(t + 1) * TILE],
                                            dst_bf[:, bass.ds(c * TPC + t, 1)].broadcast_to([P, P]),
                                            ident_bf[:, :], start=True, stop=True)
                last.then_inc(dst_spread, 1)
                pe.wait_ge(src_gathered[j], 16 * TPC * (i + 1))
                if not (first and j == 0):
                    pe.wait_ge(xt_copied, c)
                turn(xt_ps, x_src[:, j, :]).then_inc(xt_done, 1)
                pe.wait_ge(edges_loaded[j], 16 * (i + 1))
                pe.wait_ge(window_loaded[j], 16 * (i + 1))
                pe.wait_ge(onehot_done, c + 1)
                pe.wait_ge(xt_copied, c + 1)
                if not (first and j == 0):
                    pe.wait_ge(z_copied, c)
                for h in range(2):
                    cols = slice(h * HALF, (h + 1) * HALF)
                    nc.tensor.matmul(z_halves[:, h, :], w_both[:, :], feats[:, j, cols], start=True, stop=False)
                    for part in range(PARTS):
                        last = nc.tensor.matmul(z_halves[:, h, :], window[:, j, part * Z:(part + 1) * Z],
                                                onehot_t[:, j, cols], start=False, stop=part == PARTS - 1)
                last.then_inc(z_done, 1)

            with pe.If(flag(pe) < 1):
                for j in range(SLOTS):
                    chunk(0, j, True)
                with pe.Fori(1, steps) as i:
                    for j in range(SLOTS):
                        chunk(i, j, False)
                pe.wait_ge(z_done, chunks)
            with pe.Else():
                with pe.Fori(0, chunks) as c:
                    pe.wait_ge(any_gathered, (c + 1) * 2 * TPC * 16)
                    turn(xt_ps, x_src[:, 0, :])
                    turn(dst_ps, x_dst[:, :]).then_inc(any_turned, 1)
                    pe.wait_ge(any_src_copied, c + 1)
                    pe.wait_ge(any_dst_copied, c + 1)
                    pe.wait_ge(any_edges, (c + 1) * 16)
                    for h in range(2):
                        cols = slice(h * HALF, (h + 1) * HALF)
                        nc.tensor.matmul(z_halves[:, h, :], w_both[:, :], feats[:, 0, cols], start=True, stop=False)
                        last = nc.tensor.matmul(z_halves[:, h, :], w_dst[:, :], x_dst_t[:, cols],
                                                start=False, stop=True)
                    last.then_inc(any_z, 1)
                pe.wait_ge(any_z, chunks)

        @block.scalar
        def _(act):
            def table_group(i, k, first):
                n = 2 * i + k
                act.wait_ge(table_product, n + 1)
                if not first:
                    act.wait_ge(table_stored[k], 16 * i)
                nc.scalar.activation(parts[:, k, :, 0, :], pre_ps[:, k, :].rearrange("p (b z) -> p b z", z=Z),
                                     ACT.Copy).then_inc(part_hi, 1)
                act.wait_ge(part_rest, n + 1)
                nc.scalar.activation(parts[:, k, :, 1, :], rest[:, k, :].rearrange("p (b z) -> p b z", z=Z),
                                     ACT.Copy).then_inc(part_mid, 1)
                act.wait_ge(part_lo, n + 1)
                act.dma_start(table[bass.ds(n * GROUP * P, GROUP * P), :].rearrange("(b p) f -> p b f", p=P),
                              parts[:, k, :, :, :].rearrange("p b s z -> p b (s z)")).then_inc(table_stored[k], 16)

            for k in range(2):
                table_group(0, k, True)
            with act.Fori(1, groups // 2) as i:
                for k in range(2):
                    table_group(i, k, False)
            act.wait_ge(unfit_known, 1)
            act.wait_ge(consts_loaded, 16 * N_CONSTS)

            def chunk(i, j, first):
                c = i * SLOTS + j
                act.wait_ge(xt_done, c + 1)
                if not first:
                    act.wait_ge(z_done, c - SLOTS + 1)
                nc.scalar.activation(feats[0:D, j, :], xt_ps[0:D, 0:CH], ACT.Copy).then_inc(xt_copied, 1)
                act.wait_ge(z_done, c + 1)
                if not first:
                    act.wait_ge(z_stored[j], 32 * i)
                    act.wait_ge(stats_done, c - SLOTS + 1)
                nc.scalar.activation(z_out[:, j, :].rearrange("p (h n) -> p h n", n=HALF), z_halves,
                                     ACT.Identity, bias=bias[:, 0:1]).then_inc(z_copied, 1)
                act.wait_ge(z_copied, c + 1)
                act.dma_start(z_gate[bass.ds(c * D, D), :], z_out[0:D, j, :]).then_inc(z_stored[j], 16)
                act.dma_start(z_core[bass.ds(c * D, D), :], z_out[D:P, j, :]).then_inc(z_stored[j], 16)

            with act.If(flag(act) < 1):
                for j in range(SLOTS):
                    chunk(0, j, True)
                with act.Fori(1, steps) as i:
                    for j in range(SLOTS):
                        chunk(i, j, False)
                for j in range(SLOTS):
                    act.wait_ge(z_stored[j], 32 * steps)
            with act.Else():
                def any_chunk(c, first):
                    act.wait_ge(any_turned, c + 1)
                    nc.scalar.activation(feats[0:D, 0, :], xt_ps[0:D, 0:CH], ACT.Copy).then_inc(any_src_copied, 1)
                    act.wait_ge(any_z, c + 1)
                    if not first:
                        act.wait_ge(any_stored, 32 * c)
                    nc.scalar.activation(z_out[:, 0, :].rearrange("p (h n) -> p h n", n=HALF), z_halves,
                                         ACT.Identity, bias=bias[:, 0:1]).then_inc(any_z_copied, 1)

                any_chunk(0, True)
                with act.Fori(1, chunks) as c:
                    any_chunk(c, False)
                act.wait_ge(any_z_copied, chunks)



def pass2(nc, a, sem, keep, sb_in, g):
    chunks, pairs, pair_tiles, windows = g["chunks"], g["pairs"], g["pair_tiles"], g["windows"]
    blocks = g["blocks"]
    max_row, all_windows, last_rows = g["max_row"], g["all_windows"], g["last_rows"]
    z_gate, z_core = g["z_gate"], g["z_core"]
    ident, iota_row, dst_f, dst_local, base_i = g["ident"], g["iota_row"], g["dst_f"], g["dst_local"], g["base_i"]
    unfit, affine, sums = g["unfit"], g["affine"], g["sums"]
    body = 2 * PPH
    loops = pairs // body
    left = pairs - loops * body
    assert loops >= 1 and left <= PPH
    ptiles = 2 * TPC

    ctx = ExitStack()
    with ctx:
        def sb(name, shape, dt=F32):
            return sb_in(ctx, name, shape, dt)

        def ps(name, shape):
            return ctx.enter_context(nc.psum_tensor(name, shape, F32))

        gate = sb("gate", [P, 2, PPH * CH])
        core = sb("core", [P, 2, PPH * CH])
        soft = sb("soft", [P, 2, PPH * CH])
        message = sb("message", [P, 2, CH])
        onehot = sb("onehot", [P, 2, ptiles, P])
        gate_affine = sb("gate_affine", [P, 2])
        core_affine = sb("core_affine", [P, 2])
        any_local = sb("any_local", [P, TPC])
        turn_ps = ps("turn_ps", [P, 2, 2 * BANK])
        sum_ps = ps("sum_ps", [P, 2, BANK])

        affine_loaded = sem("affine_loaded")
        sums_zero = sem("sums_zero")
        gate_loaded = [sem(f"gate_loaded{s}") for s in range(2)]
        core_loaded = [sem(f"core_loaded{s}") for s in range(2)]
        sigmoid_done = sem("sigmoid_done")
        exp_done = sem("exp_done")
        log_done = sem("log_done")
        norms_due = sem("norms_due")
        normed = sem("normed")
        softplus_done = sem("softplus_done")
        product_done = sem("product_done")
        turned = sem("turned")
        message_copied = sem("message_copied")
        onehot_made = sem("onehot_made")
        summed = sem("summed")
        sums_added = sem("sums_added")
        any_pair = sem("any_pair")
        any_local_made = sem("any_local_made")
        any_onehot = sem("any_onehot")
        any_summed = sem("any_summed")
        any_added = sem("any_added")

        block = ctx.enter_context(nc.Block())

        def flag(eng):
            return eng.value_load(unfit[0:1, 0:1], min_val=0, max_val=1)

        @block.sync
        def _(sp):
            for h in range(2):
                rows = slice(h * D, (h + 1) * D)
                sp.dma_start(gate_affine[rows, :], affine[0:D, :]).then_inc(affine_loaded, 16)
                sp.dma_start(core_affine[rows, :], affine[D:P, :]).then_inc(affine_loaded, 16)

            def load_half(i, s, n, first):
                half = 2 * i + s
                if not first:
                    sp.wait_ge(product_done, (half - 1) * PPH)
                for buf, z, done in ((gate, z_gate, gate_loaded), (core, z_core, core_loaded)):
                    sp.dma_start(buf[:, s, 0:n * CH].rearrange("p (k n) -> p k n", n=CH),
                                 z[bass.ds(half * PPH * P, n * P), :].rearrange("(k p) n -> p k n", p=P))\
                        .then_inc(done[s], 16)

            with sp.If(flag(sp) < 1):
                for s in range(2):
                    load_half(0, s, PPH, True)
                with sp.Fori(1, loops) as i:
                    for s in range(2):
                        load_half(i, s, PPH, False)
                if left:
                    load_half(loops, 0, left, False)
                sp.wait_ge(product_done, pairs)
            with sp.Else():
                def any_load(u, first):
                    if not first:
                        sp.wait_ge(any_pair, u)
                    sp.dma_start(gate[:, 0, 0:CH], z_gate[bass.ds(u * P, P), :]).then_inc(gate_loaded[0], 16)
                    sp.dma_start(core[:, 0, 0:CH], z_core[bass.ds(u * P, P), :]).then_inc(core_loaded[0], 16)

                any_load(0, True)
                with sp.Fori(1, pairs) as u:
                    any_load(u, False)
                sp.wait_ge(any_pair, pairs)
            sp.wait_ge(affine_loaded, 64)

        @block.scalar
        def _(act):
            act.wait_ge(affine_loaded, 64)

            def gates(s, n):
                cols = slice(0, n * CH)
                nc.scalar.activation(gate[:, s, cols], gate[:, s, cols], ACT.Sigmoid,
                                     bias=gate_affine[:, 1:2], scale=gate_affine[:, 0:1]).then_inc(sigmoid_done, 1)

            def exps(s, n):
                cols = slice(0, n * CH)
                nc.scalar.activation(soft[:, s, cols], core[:, s, cols], ACT.Exp,
                                     bias=core_affine[:, 1:2], scale=core_affine[:, 0:1]).then_inc(exp_done, 1)

            def logs(s, n):
                cols = slice(0, n * CH)
                nc.scalar.activation(soft[:, s, cols], soft[:, s, cols], ACT.Ln, bias=1.0).then_inc(log_done, 1)

            def half(i, s, n, first):
                number = 2 * i + s
                act.wait_ge(gate_loaded[s], 16 * (i + 1))
                gates(s, n)
                act.wait_ge(core_loaded[s], 16 * (i + 1))
                if not first:
                    act.wait_ge(turned, (number - 1) * PPH)
                exps(s, n)
                act.wait_ge(exp_done, number + 1)
                logs(s, n)

            with act.If(flag(act) < 1):
                for s in range(2):
                    half(0, s, PPH, True)
                with act.Fori(1, loops) as i:
                    for s in range(2):
                        half(i, s, PPH, False)
                if left:
                    half(loops, 0, left, False)
                act.wait_ge(log_done, 2 * loops + (left > 0))
            with act.Else():
                with act.Fori(0, pairs) as u:
                    act.wait_ge(gate_loaded[0], 16 * (u + 1))
                    gates(0, 1)
                    act.wait_ge(core_loaded[0], 16 * (u + 1))
                    exps(0, 1)
                    act.wait_ge(exp_done, u + 1)
                    logs(0, 1)
                act.wait_ge(log_done, pairs)

        @block.gpsimd
        def _(pool):
            pool.wait_ge(affine_loaded, 64)

            def norm(s, n):
                pool.sem_inc(norms_due, 1)
                cols = slice(0, n * CH)
                nc.gpsimd.tensor_scalar(core[:, s, cols], core[:, s, cols], core_affine[:, 0:1],
                                        core_affine[:, 1:2], ALU.mult, ALU.add).then_inc(normed, 1)

            with pool.If(flag(pool) < 1):
                for s in range(2):
                    pool.wait_ge(exp_done, s + 1)
                    norm(s, PPH)
                with pool.Fori(1, loops) as i:
                    for s in range(2):
                        pool.wait_ge(exp_done, 2 * i + s + 1)
                        norm(s, PPH)
                if left:
                    pool.wait_ge(exp_done, 2 * loops + 1)
                    norm(0, left)
            with pool.Else():
                with pool.Fori(0, pairs) as u:
                    pool.wait_ge(exp_done, u + 1)
                    norm(0, 1)
            pool.wait_ge(sums_zero, 1)

        @block.vector
        def _(dve):
            nc.vector.memset(sums[:, :], 0.0).then_inc(sums_zero, 1)
            dve.wait_ge(affine_loaded, 64)
            dve.wait_ge(sums_zero, 1)

            iota_many = iota_row[:, :].unsqueeze(1).broadcast_to([P, ptiles, P])

            def mark(u, r, first):
                if not first:
                    dve.wait_ge(summed, u - 1)
                nc.vector.tensor_tensor(
                    onehot[:, r, :, :], iota_many,
                    dst_local[:, bass.ds(u * ptiles, ptiles)].unsqueeze(2).broadcast_to([P, ptiles, P]),
                    ALU.is_equal).then_inc(onehot_made, 1)

            def combine(s, k, u, half):
                cols = slice(k * CH, (k + 1) * CH)
                dve.wait_ge(normed, half)
                dve.wait_ge(log_done, half)
                nc.vector.scalar_tensor_tensor(out=soft[:, s, cols], in0=soft[:, s, cols], scalar=SP_CAP,
                                               in1=core[:, s, cols], op0=ALU.min, op1=ALU.max)\
                    .then_inc(softplus_done, 1)
                dve.wait_ge(softplus_done, u + 1)
                dve.wait_ge(sigmoid_done, half)
                nc.vector.tensor_tensor(soft[:, s, cols], soft[:, s, cols], gate[:, s, cols], ALU.mult)\
                    .then_inc(product_done, 1)

            def copy_message(u, r, first):
                dve.wait_ge(turned, u + 1)
                if not first:
                    dve.wait_ge(summed, u - 1)
                nc.vector.tensor_copy(message[:, r, :], turn_ps[:, r, 0:CH]).then_inc(message_copied, 1)

            def add_sums(u, r, first):
                dve.wait_ge(summed, u + 1)
                for h in range(2):
                    row = dve.value_load(base_i[0:1, bass.ds(2 * u + h, 1)], min_val=0, max_val=max_row)
                    if not (first and h == 0):
                        dve.wait_ge(sums_added, 2 * u + h)
                    nc.vector.tensor_tensor(sums[:, bass.ds(row, D)], sums[:, bass.ds(row, D)],
                                            sum_ps[:, r, h * D:(h + 1) * D], ALU.add).then_inc(sums_added, 1)

            def pair(i, k, first):
                u = i * body + k
                s, p = divmod(k, PPH)
                mark(u, k % 2, first and k < 2)
                combine(s, p, u, 2 * i + s + 1)
                if not (first and k < 1):
                    copy_message(u - 1, (k - 1) % 2, first and k < 3)
                if not (first and k < 2):
                    add_sums(u - 2, k % 2, first and k == 2)

            with dve.If(flag(dve) < 1):
                for k in range(body):
                    pair(0, k, True)
                with dve.Fori(1, loops) as i:
                    for k in range(body):
                        pair(i, k, False)
                for k in range(left):
                    pair(loops, k, False)
                copy_message(pairs - 1, (pairs - 1) % 2, False)
                for u in range(pairs - 2, pairs):
                    add_sums(u, u % 2, False)
                dve.wait_ge(sums_added, 2 * pairs)
            with dve.Else():
                def any_window(u, h, w, first):
                    n = (2 * u + h) * all_windows + w
                    dve.wait_ge(any_local_made, n + 2 * u + h + 1)
                    nc.vector.tensor_tensor(
                        onehot[:, 0, 0:TPC, :], iota_row[:, :].unsqueeze(1).broadcast_to([P, TPC, P]),
                        any_local[:, :].unsqueeze(2).broadcast_to([P, TPC, P]), ALU.is_equal)\
                        .then_inc(any_onehot, 1)
                    dve.wait_ge(any_onehot, n + 1)
                    nc.vector.tensor_scalar(any_local[:, :], any_local[:, :], float(P), None, ALU.subtract)\
                        .then_inc(any_local_made, 1)
                    dve.wait_ge(any_summed, n + 1)
                    nc.vector.tensor_tensor(sums[:, bass.ds(w * P, D)], sums[:, bass.ds(w * P, D)],
                                            sum_ps[:, 0, 0:D], ALU.add).then_inc(any_added, 1)

                def any_pair_step(u):
                    combine(0, 0, u, u + 1)
                    dve.wait_ge(turned, u + 1)
                    nc.vector.tensor_copy(message[:, 0, :], turn_ps[:, 0, 0:CH]).then_inc(message_copied, 1)
                    for h in range(2):
                        if h:
                            dve.wait_ge(any_local_made, (2 * u + h) * (all_windows + 1))
                        nc.vector.tensor_copy(any_local[:, :], dst_f[:, bass.ds((2 * u + h) * TPC, TPC)])\
                            .then_inc(any_local_made, 1)
                        with dve.Fori(0, all_windows) as w:
                            any_window(u, h, w, False)
                    dve.wait_ge(any_added, (2 * u + 2) * all_windows)
                    nc.vector.memset(onehot[:, 1, 0, 0:1], 0.0).then_inc(any_pair, 1)
                    dve.wait_ge(any_pair, u + 1)
                    dve.wait_ge(any_local_made, (2 * u + 2) * (all_windows + 1))

                with dve.Fori(0, pairs) as u:
                    any_pair_step(u)
                dve.wait_ge(any_pair, pairs)

        @block.tensor
        def _(pe):
            def turn(s, k, r):
                for t in range(TPC):
                    at = k * CH + t * TILE
                    last = nc.tensor.transpose(turn_ps[:, r, t * P:(t + 1) * P], soft[:, s, at:at + TILE],
                                               ident[:, :])
                last.then_inc(turned, 1)

            def turn_pair(u, s, k, r, first):
                pe.wait_ge(product_done, u + 1)
                if not first:
                    pe.wait_ge(message_copied, u - 1)
                turn(s, k, r)

            def sum_pair(u, r, first):
                pe.wait_ge(message_copied, u + 1)
                pe.wait_ge(onehot_made, u + 1)
                if not first:
                    pe.wait_ge(sums_added, 2 * u - 2)
                for h in range(2):
                    for t in range(TPC):
                        last = nc.tensor.matmul(sum_ps[:, r, h * D:(h + 1) * D], onehot[:, r, h * TPC + t, :],
                                                message[:, r, t * P + h * D:t * P + (h + 1) * D],
                                                start=t == 0, stop=t == TPC - 1)
                last.then_inc(summed, 1)

            def pair(i, k, first):
                u = i * body + k
                s, p = divmod(k, PPH)
                turn_pair(u, s, p, k % 2, first and k < 2)
                if not (first and k < 1):
                    sum_pair(u - 1, (k - 1) % 2, first and k < 3)

            with pe.If(flag(pe) < 1):
                for k in range(body):
                    pair(0, k, True)
                with pe.Fori(1, loops) as i:
                    for k in range(body):
                        pair(i, k, False)
                for k in range(left):
                    pair(loops, k, False)
                sum_pair(pairs - 1, (pairs - 1) % 2, False)
                pe.wait_ge(summed, pairs)
            with pe.Else():
                with pe.Fori(0, pairs) as u:
                    pe.wait_ge(product_done, u + 1)
                    turn(0, 0, 0)
                    for h in range(2):
                        with pe.Fori(0, all_windows) as w:
                            pe.wait_ge(message_copied, u + 1)
                            pe.wait_ge(any_onehot, (2 * u + h) * all_windows + w + 1)
                            for t in range(TPC):
                                last = nc.tensor.matmul(sum_ps[:, 0, 0:D], onehot[:, 0, t, :],
                                                        message[:, 0, t * P + h * D:t * P + (h + 1) * D],
                                                        start=t == 0, stop=t == TPC - 1)
                            last.then_inc(any_summed, 1)
                pe.wait_ge(any_summed, 2 * pairs * all_windows)


def nodes(nc, a, out, sem, keep, sb_in, g):
    blocks, windows, last_rows = g["blocks"], g["windows"], g["last_rows"]
    n_nodes = a["x"].shape[0]
    sums, ident = g["sums"], g["ident"]
    full = blocks - 1
    per = 7
    assert per * D <= BANK and blocks % per == 0
    rounds = blocks // per
    even = -(-windows // 2)

    ctx = ExitStack()
    with ctx:
        def sb(name, shape, dt=F32):
            return sb_in(ctx, name, shape, dt)

        def ps(name, shape):
            return ctx.enter_context(nc.psum_tensor(name, shape, F32))

        x_nodes = sb("x_nodes", [P, blocks, D])
        shifted = sb("shifted", [P, blocks, D])
        update = sb("update", [P, blocks, D])
        work = sb("work", [P, blocks, D])
        ones = sb("ones", [P, P])
        tail_ones = sb("tail_ones", [P, P])
        bn2 = sb("bn2", [P, 2, D])
        mean = sb("mean", [P, D])
        var = sb("var", [P, D])
        power = sb("power", [P, max(blocks, D)])
        row_mean = sb("row_mean", [P, blocks])
        row_var = sb("row_var", [P, blocks])
        mean_ps = ps("mean_ps", [P, BANK])
        var_ps = ps("var_ps", [P, BANK])

        loaded = sem("nodes_loaded")
        shifted_zero = sem("shifted_zero")
        shifted_loaded = sem("shifted_loaded")
        dve_step = sem("node_dve_step")
        col_sums = sem("col_sums")
        squared = sem("squared")
        sq_sums = sem("sq_sums")
        power_done = sem("power_done")
        exp_done = sem("node_exp_done")
        log_done = sem("node_log_done")
        row_squared = sem("row_squared")
        out_ready = sem("out_ready")
        out_stored = sem("out_stored")
        block = ctx.enter_context(nc.Block())

        def over_nodes(t):
            return t[:, :].unsqueeze(1).broadcast_to([P, blocks, D])

        def over_channels(t):
            return t[:, :].unsqueeze(2).broadcast_to([P, blocks, D])

        by_window = sums[:, :].rearrange("p (b o d) -> p b o d", o=2, d=D)

        @block.sync
        def _(sp):
            sp.wait_ge(shifted_zero, 1)
            sp.dma_start(shifted[0:D, 1:blocks, :], by_window[D:P, 0:blocks - 1, 1, :]).then_inc(shifted_loaded, 16)
            sp.dma_start(shifted[D:P, :, :], by_window[0:D, :, 1, :]).then_inc(shifted_loaded, 16)
            sp.dma_start(x_nodes[:, 0:full, :], a["x"][0:full * P, :].rearrange("(b p) d -> p b d", p=P))\
                .then_inc(loaded, 16)
            sp.wait_ge(dve_step, 1)
            sp.dma_start(x_nodes[0:last_rows, full, :], a["x"][full * P:n_nodes, :]).then_inc(loaded, 16)
            sp.wait_ge(out_ready, 1)
            sp.dma_start(out[0:full * P, :].rearrange("(b p) d -> p b d", p=P), update[:, 0:full, :])\
                .then_inc(out_stored, 16)
            sp.dma_start(out[full * P:n_nodes, :], update[0:last_rows, full, :]).then_inc(out_stored, 16)
            sp.wait_ge(out_stored, 32)

        @block.scalar
        def _(act):
            act.dma_start(bn2[:, 0, :], a["gamma2"].broadcast_to([P, D])).then_inc(loaded, 16)
            act.dma_start(bn2[:, 1, :], a["beta2"].broadcast_to([P, D])).then_inc(loaded, 16)
            act.dma_start(tail_ones[:, :], a["tail_ones"]).then_inc(loaded, 16)
            act.wait_ge(dve_step, 5)
            nc.scalar.activation(work[:, :, :], update[:, :, :], ACT.Square).then_inc(squared, 1)
            act.wait_ge(dve_step, 12)
            nc.scalar.activation(work[:, :, :], work[:, :, :], ACT.Exp).then_inc(exp_done, 1)
            act.wait_ge(exp_done, 1)
            nc.scalar.activation(work[:, :, :], work[:, :, :], ACT.Ln, bias=1.0).then_inc(log_done, 1)
            act.wait_ge(dve_step, 17)
            nc.scalar.activation(work[:, :, :], update[:, :, :], ACT.Square).then_inc(row_squared, 1)
            act.wait_ge(row_squared, 1)

        @block.gpsimd
        def _(pool):
            nc.gpsimd.memset(power[:, :], -0.5).then_inc(power_done, 1)
            pool.wait_ge(power_done, 1)
            pool.wait_ge(dve_step, 7)
            nc.gpsimd.tensor_tensor(var[:, :], var[:, :], power[:, 0:D], ALU.pow).then_inc(power_done, 1)
            pool.wait_ge(dve_step, 19)
            nc.gpsimd.tensor_tensor(row_var[:, :], row_var[:, :], power[:, 0:blocks], ALU.pow).then_inc(power_done, 1)
            pool.wait_ge(power_done, 3)

        @block.tensor
        def _(pe):
            def column_sums(to, rows, tail):
                for r in range(rounds):
                    n = per - (r == rounds - 1)
                    last = nc.tensor.matmul(to[:, 0:n * D], ones[:, :],
                                            rows[:, r * per:r * per + n, :].rearrange("p b d -> p (b d)"),
                                            start=r == 0, stop=False)
                return nc.tensor.matmul(to[:, (per - 1) * D:per * D], tail[:, :], rows[:, full, :],
                                        start=False, stop=True)

            pe.wait_ge(loaded, 16 * 5)
            pe.wait_ge(dve_step, 3)
            column_sums(mean_ps, update, tail_ones).then_inc(col_sums, 1)
            pe.wait_ge(squared, 1)
            column_sums(var_ps, work, tail_ones).then_inc(sq_sums, 1)

        @block.vector
        def _(dve):
            done = [0]

            def step(ins):
                done[0] += 1
                ins.then_inc(dve_step, 1)
                dve.wait_ge(dve_step, done[0])

            nc.vector.memset(shifted[0:D, 0, :], 0.0).then_inc(shifted_zero, 1)
            step(nc.vector.memset(x_nodes[:, full, :], 0.0))
            step(nc.vector.memset(ones[:, :], 1.0))
            dve.wait_ge(shifted_zero, 1)
            dve.wait_ge(shifted_loaded, 32)
            step(nc.vector.tensor_tensor(update[:, :, :], by_window[:, :, 0, :], shifted[:, :, :], ALU.add))
            dve.wait_ge(col_sums, 1)
            step(nc.vector.tensor_reduce(mean[:, :], mean_ps[:, 0:per * D].rearrange("p (b d) -> p d b", d=D),
                                         AX_X, ALU.add))
            nc.vector.tensor_scalar(mean[:, :], mean[:, :], 1.0 / n_nodes, None, ALU.mult).then_inc(shifted_zero, 1)
            dve.wait_ge(shifted_zero, 2)
            step(nc.vector.tensor_tensor(update[:, :, :], update[:, :, :], over_nodes(mean), ALU.subtract))
            dve.wait_ge(sq_sums, 1)
            step(nc.vector.tensor_reduce(var[:, :], var_ps[:, 0:per * D].rearrange("p (b d) -> p d b", d=D),
                                         AX_X, ALU.add))
            step(nc.vector.tensor_scalar(var[:, :], var[:, :], 1.0 / n_nodes, EPS, ALU.mult, ALU.add))
            dve.wait_ge(power_done, 2)
            dve.wait_ge(loaded, 16 * 5)
            step(nc.vector.tensor_tensor(var[:, :], var[:, :], bn2[:, 0, :], ALU.mult))
            step(nc.vector.tensor_tensor(update[:, :, :], update[:, :, :], over_nodes(var), ALU.mult))
            step(nc.vector.tensor_tensor(update[:, :, :], update[:, :, :],
                                         bn2[:, 1, :].unsqueeze(1).broadcast_to([P, blocks, D]), ALU.add))
            step(nc.vector.tensor_tensor(update[:, :, :], update[:, :, :], x_nodes[:, :, :], ALU.add))
            step(nc.vector.tensor_scalar(work[:, :, :], update[:, :, :], SP_CAP, None, ALU.min))
            dve.wait_ge(log_done, 1)
            step(nc.vector.tensor_tensor(work[:, :, :], work[:, :, :], update[:, :, :], ALU.max))
            step(nc.vector.tensor_tensor(update[:, :, :], work[:, :, :], x_nodes[:, :, :], ALU.add))
            step(nc.vector.tensor_reduce(row_mean[:, :], update[:, :, :], AX_X, ALU.add))
            step(nc.vector.tensor_scalar(row_mean[:, :], row_mean[:, :], 1.0 / D, None, ALU.mult))
            step(nc.vector.tensor_tensor(update[:, :, :], update[:, :, :], over_channels(row_mean), ALU.subtract))
            dve.wait_ge(row_squared, 1)
            step(nc.vector.tensor_reduce(row_var[:, :], work[:, :, :], AX_X, ALU.add))
            step(nc.vector.tensor_scalar(row_var[:, :], row_var[:, :], 1.0 / D, EPS, ALU.mult, ALU.add))
            dve.wait_ge(power_done, 3)
            nc.vector.tensor_tensor(update[:, :, :], update[:, :, :], over_channels(row_var), ALU.mult)\
                .then_inc(out_ready, 1)
            dve.wait_ge(out_ready, 1)


def kernel(**inputs):
    import concourse.bacc as bacc
    from concourse.bass_utils import run_bass_kernel_spmd

    x = np.asarray(inputs["x"])
    src = np.asarray(inputs["src"])
    dst = np.asarray(inputs["dst"])
    edges = np.asarray(inputs["edge_attr_64"])
    n_nodes, n_edges = x.shape[0], src.shape[0]
    chunks, blocks, windows, groups, pairs = sizes(n_nodes, n_edges)

    x_t = np.zeros((D, groups * GROUP * P), x.dtype)
    x_t[:, :n_nodes] = x.T
    iota = np.arange(P, dtype=np.float32)
    tail = np.zeros((P, P), np.float32)
    tail[:n_nodes - (blocks - 1) * P, :] = 1.0
    arrays = {
        "x": x,
        "x_groups": np.ascontiguousarray(x_t.reshape(D, groups, GROUP * P).transpose(1, 0, 2)).reshape(-1, GROUP * P),
        "src_cols": np.ascontiguousarray(src.reshape(-1, TILE).T),
        "dst_cols": np.ascontiguousarray(dst.reshape(-1, TILE).T),
        "edge_chunks": np.ascontiguousarray(edges.reshape(chunks, CH, D).transpose(0, 2, 1)).reshape(-1, CH),
        "w": np.asarray(inputs["L0_gnn_W"]),
        "b": np.asarray(inputs["L0_gnn_b"]).reshape(Z, 1),
        "gamma1": np.asarray(inputs["L0_gnn_bn1_gamma"]).reshape(Z, 1),
        "beta1": np.asarray(inputs["L0_gnn_bn1_beta"]).reshape(Z, 1),
        "gamma2": np.asarray(inputs["L0_gnn_bn2_gamma"]).reshape(1, D),
        "beta2": np.asarray(inputs["L0_gnn_bn2_beta"]).reshape(1, D),
        "ident": np.eye(P, dtype=np.float32),
        "iota_row": np.tile(iota, (P, 1)),
        "iota_col": iota.reshape(P, 1).copy(),
        "tail_ones": tail,
    }
    nc = bacc.Bacc("TRN2", target_bir_lowering=False, num_devices=1)
    aps = {name: nc.dram_tensor(f"in_{name}", v.shape, mybir.dt.from_np(v.dtype), kind="ExternalInput").ap()
           for name, v in arrays.items()}
    out = nc.dram_tensor("out", (n_nodes, D), F32, kind="ExternalOutput").ap()
    build_program(nc, aps, out)
    got = run_bass_kernel_spmd(nc, [{f"in_{name}": v for name, v in arrays.items()}], core_ids=[0])
    return got.results[0]["out"]
```

```python
from contextlib import ExitStack

import numpy as np

import concourse.bass as bass
from concourse import mybir

F32 = mybir.dt.float32
BF16 = mybir.dt.bfloat16
I32 = mybir.dt.int32
ALU = mybir.AluOpType
ACT = mybir.ActivationFunctionType
AX_X = mybir.AxisListType.X

P = 128
D = 64
Z = 2 * D
TILE = 128
TPC = 5
CH = TPC * TILE
HALF = CH // 2
BANK = 512
SLOTS = 5
WIN = 64
PARTS = 3
GROUP = 4
PPH = 6
PIECE = 2
EPS = 1e-5
EXP_LN_SET = "natural_log_exp_and_others"
SP_CAP = 30.0


def sizes(n_nodes, n_edges):
    chunks = n_edges // CH
    assert chunks * CH == n_edges and chunks % SLOTS == 0
    blocks = -(-n_nodes // P)
    groups = -(-(n_nodes - 1 + WIN) // (GROUP * P))
    groups += groups % 2
    pairs = -(-chunks // 2)
    return chunks, blocks, groups, pairs


def build_program(nc, a, out):
    n_nodes = a["x"].shape[0]
    n_edges = a["src_cols"].shape[1] * TILE
    chunks, blocks, groups, pairs = sizes(n_nodes, n_edges)
    tiles = chunks * TPC
    pair_tiles = 2 * pairs * TPC
    steps = chunks // SLOTS
    max_row = n_nodes - 1
    node_cols = max(blocks * P, n_nodes + WIN)
    idx_groups = -(-chunks // P)
    assert chunks % idx_groups == 0 and n_nodes % 2 == 0
    per_group = chunks // idx_groups

    table = nc.dram_tensor("dst_table", (groups * GROUP * P, PARTS * Z), BF16, kind="Internal").ap()
    z_gate = nc.dram_tensor("z_gate", (2 * pairs * D, CH), F32, kind="Internal").ap()
    z_core = nc.dram_tensor("z_core", (2 * pairs * D, CH), F32, kind="Internal").ap()

    keep = ExitStack()
    with keep:
        def sb_in(ctx, name, shape, dt=F32):
            return ctx.enter_context(nc.sbuf_tensor(name, shape, dt))

        def sem(name):
            return keep.enter_context(nc.semaphore(name))

        ident = sb_in(keep, "ident", [P, P])
        iota_row = sb_in(keep, "iota_row", [P, P])
        dst_f = sb_in(keep, "dst_f", [P, pair_tiles])
        dst_local = sb_in(keep, "dst_local", [P, pair_tiles])
        base_i = sb_in(keep, "base_i", [P, 2 * pairs], I32)
        unfit = sb_in(keep, "unfit", [1, 1], I32)
        affine = sb_in(keep, "affine", [P, 2])

        pass1(nc, a, sem, keep, sb_in, locals())
        sums = sb_in(keep, "sums", [P, node_cols])
        pass2(nc, a, sem, keep, sb_in, locals())
        nodes(nc, a, out, sem, keep, sb_in, locals())
    return nc


def pass1(nc, a, sem, keep, sb_in, g):
    chunks, groups, pairs, tiles, steps = g["chunks"], g["groups"], g["pairs"], g["tiles"], g["steps"]
    pair_tiles, max_row, idx_groups, per_group = g["pair_tiles"], g["max_row"], g["idx_groups"], g["per_group"]
    table, z_gate, z_core = g["table"], g["z_gate"], g["z_core"]
    ident, iota_row, dst_f, dst_local, base_i = g["ident"], g["iota_row"], g["dst_f"], g["dst_local"], g["base_i"]
    unfit, affine = g["unfit"], g["affine"]
    halves = 2 * chunks

    ctx = ExitStack()
    with ctx:
        def sb(name, shape, dt=F32):
            return sb_in(ctx, name, shape, dt)

        def ps(name, shape):
            return ctx.enter_context(nc.psum_tensor(name, shape, F32))

        ident_bf = sb("ident_bf", [P, P], BF16)
        iota_col = sb("iota_col", [P, 1])
        w_both = sb("w_both", [P, Z])
        w_dst = sb("w_dst", [D, Z])
        bias = sb("bias", [P, 1])
        bn1 = sb("bn1", [P, 2])
        src_all = sb("src_all", [P, tiles + SLOTS * TPC], I32)
        dst_i = sb("dst_i", [P, tiles], I32)
        dst_bf = sb("dst_bf", [P, tiles], BF16)
        least = sb("least", [P, chunks])
        least_t = sb("least_t", [P, idx_groups])
        base_f = sb("base_f", [P, chunks])
        top = sb("top", [P, 1])
        top_one = sb("top_one", [1, 4])
        x_group = sb("x_group", [D, 2, GROUP * P])
        rest = sb("rest", [P, 2, GROUP * Z])
        parts = sb("parts", [P, 2, GROUP, PARTS, Z], BF16)
        src_idx = sb("src_idx", [P, SLOTS, TPC], I32)
        dst_idx = sb("dst_idx", [P, TPC], I32)
        x_src = sb("x_src", [P, SLOTS, TPC * D])
        x_dst = sb("x_dst", [P, TPC * D])
        feats = sb("feats", [P, SLOTS, CH])
        x_dst_t = sb("x_dst_t", [D, CH])
        window = sb("window", [WIN, SLOTS, PARTS * Z], BF16)
        onehot_t = sb("onehot_t", [WIN, SLOTS, CH], BF16)
        z_out = sb("z_out", [P, SLOTS, CH])
        stats = sb("stats", [P, 6 * halves])
        moments = sb("moments", [P, 2])
        small = sb("small", [P, 4])
        zero = sb("zero", [D, CH])

        xt_ps = ps("xt_ps", [P, 2 * BANK])
        dst_ps = ps("dst_ps", [P, 2 * BANK])
        z_ps = ps("z_ps", [P, 2 * BANK])
        pre_ps = ps("pre_ps", [P, 2, BANK])
        z_halves = z_ps[:, :].rearrange("p (h n) -> p h n", n=BANK)[:, :, 0:HALF]

        consts_loaded = sem("consts_loaded")
        src_loaded = sem("src_loaded")
        dst_loaded = sem("dst_loaded")
        zero_made = sem("zero_made")
        pad_stored = sem("pad_stored")
        x_group_loaded = [sem(f"x_group_loaded{k}") for k in range(2)]
        window_step = sem("window_step")
        least_moved = sem("least_moved")
        least_spread = sem("least_spread")
        top_moved = sem("top_moved")
        unfit_known = sem("unfit_known")
        table_product = sem("table_product")
        part_hi = sem("part_hi")
        part_rest = sem("part_rest")
        part_mid = sem("part_mid")
        part_lo = sem("part_lo")
        table_stored = [sem(f"table_stored{k}") for k in range(2)]
        ident_cast = sem("ident_cast")
        idx_copied = sem("idx_copied")
        src_gathered = [sem(f"src_gathered{j}") for j in range(SLOTS)]
        gathers_due = sem("gathers_due")
        turns_due = sem("turns_due")
        dst_spread = sem("dst_spread")
        onehot_done = sem("onehot_done")
        xt_done = sem("xt_done")
        xt_copied = sem("xt_copied")
        edges_loaded = [sem(f"edges_loaded{j}") for j in range(SLOTS)]
        window_loaded = [sem(f"window_loaded{j}") for j in range(SLOTS)]
        z_done = sem("z_done")
        z_copied = sem("z_copied")
        stats_done = sem("stats_done")
        z_stored = [sem(f"z_stored{j}") for j in range(SLOTS)]
        affine_step = sem("affine_step")
        any_idx = sem("any_idx")
        any_gathered = sem("any_gathered")
        any_turned = sem("any_turned")
        any_src_copied = sem("any_src_copied")
        any_dst_copied = sem("any_dst_copied")
        any_edges = sem("any_edges")
        any_z = sem("any_z")
        any_z_copied = sem("any_z_copied")
        any_stats = sem("any_stats")
        any_stored = sem("any_stored")

        block = ctx.enter_context(nc.Block())
        N_CONSTS = 9

        def flag(eng):
            return eng.value_load(unfit[0:1, 0:1], min_val=0, max_val=1)

        @block.sync
        def _(sp):
            sp.dma_start(dst_i[:, :], a["dst_cols"]).then_inc(dst_loaded, 16)
            sp.dma_start(ident[:, :], a["ident"]).then_inc(consts_loaded, 16)
            sp.dma_start(iota_row[:, :], a["iota_row"]).then_inc(consts_loaded, 16)
            sp.dma_start(iota_col[:, :], a["iota_col"]).then_inc(consts_loaded, 16)
            sp.dma_start(w_both[0:D, :], a["w"][0:D, :]).then_inc(consts_loaded, 16)
            sp.dma_start(w_both[D:P, :], a["w"][2 * D:3 * D, :]).then_inc(consts_loaded, 16)
            sp.dma_start(w_dst[:, :], a["w"][D:2 * D, :]).then_inc(consts_loaded, 16)
            sp.dma_start(bias[:, :], a["b"]).then_inc(consts_loaded, 16)
            sp.dma_start(bn1[:, 0:1], a["gamma1"]).then_inc(consts_loaded, 16)
            sp.dma_start(bn1[:, 1:2], a["beta1"]).then_inc(consts_loaded, 16)
            sp.dma_start(src_all[:, 0:tiles], a["src_cols"]).then_inc(src_loaded, 16)
            for k in range(2):
                sp.dma_start(x_group[:, k, :], a["x_groups"][k * D:(k + 1) * D, :]).then_inc(x_group_loaded[k], 16)
            with sp.Fori(1, groups // 2) as i:
                for k in range(2):
                    sp.wait_ge(table_product, 2 * i + k - 1)
                    sp.dma_start(x_group[:, k, :], a["x_groups"][bass.ds((2 * i + k) * D, D), :])\
                        .then_inc(x_group_loaded[k], 16)
            if 2 * pairs > chunks:
                sp.wait_ge(zero_made, 1)
                sp.dma_start(z_gate[chunks * D:, :], zero[:, :]).then_inc(pad_stored, 16)
                sp.dma_start(z_core[chunks * D:, :], zero[:, :]).then_inc(pad_stored, 16)
            for k in range(2):
                sp.wait_ge(table_stored[k], 16 * (groups // 2))
            sp.wait_ge(unfit_known, 1)

            def load_chunk(i, j, first):
                c = i * SLOTS + j
                if not first:
                    sp.wait_ge(z_done, c - SLOTS + 1)
                sp.dma_start(feats[D:P, j, :], a["edge_chunks"][bass.ds(c * D, D), :]).then_inc(edges_loaded[j], 16)
                row = sp.value_load(base_i[0:1, bass.ds(c, 1)], min_val=0, max_val=max_row)
                sp.dma_start(window[:, j, :], table[bass.ds(row, WIN), :]).then_inc(window_loaded[j], 16)

            with sp.If(flag(sp) < 1):
                for j in range(SLOTS):
                    load_chunk(0, j, True)
                with sp.Fori(1, steps) as i:
                    for j in range(SLOTS):
                        load_chunk(i, j, False)
            with sp.Else():
                with sp.Fori(0, chunks) as c:
                    sp.wait_ge(any_idx, c + 1)
                    sp.dma_start(feats[D:P, 0, :], a["edge_chunks"][bass.ds(c * D, D), :]).then_inc(any_edges, 16)
                    sp.wait_ge(any_z_copied, c + 1)
                    sp.dma_start(z_gate[bass.ds(c * D, D), :], z_out[0:D, 0, :]).then_inc(any_stored, 16)
                    sp.dma_start(z_core[bass.ds(c * D, D), :], z_out[D:P, 0, :]).then_inc(any_stored, 16)
                sp.wait_ge(any_stored, 32 * chunks)
            if 2 * pairs > chunks:
                sp.wait_ge(pad_stored, 32)

        @block.gpsimd
        def _(pool):
            nc.gpsimd.memset(zero[:, :], 0.0).then_inc(zero_made, 1)
            pool.wait_ge(unfit_known, 1)

            def gather(rows, idx, done):
                pool.sem_inc(gathers_due, 1)
                for t in range(TPC):
                    pool.indirect_dma_start(
                        rows[:, t * D:(t + 1) * D], None, a["x"],
                        bass.IndirectOffsetOnAxis(ap=idx[:, t:t + 1], axis=0)).then_inc(done, 16)

            def gather_chunk(i, j, first):
                c = i * SLOTS + j
                pool.wait_ge(idx_copied, c + 1)
                if not first:
                    pool.wait_ge(xt_done, c - SLOTS + 1)
                gather(x_src[:, j, :], src_idx[:, j, :], src_gathered[j])

            with pool.If(flag(pool) < 1):
                for j in range(SLOTS):
                    gather_chunk(0, j, True)
                with pool.Fori(1, steps) as i:
                    for j in range(SLOTS):
                        gather_chunk(i, j, False)
            with pool.Else():
                with pool.Fori(0, chunks) as c:
                    pool.wait_ge(any_idx, c + 1)
                    gather(x_src[:, 0, :], src_idx[:, 0, :], any_gathered)
                    gather(x_dst[:, :], dst_idx[:, :], any_gathered)
            pool.wait_ge(affine_step, 3)
            nc.gpsimd.tensor_tensor(small[:, 2:3], small[:, 0:1], small[:, 1:2], ALU.pow).then_inc(affine_step, 1)

        @block.vector
        def _(dve):
            done = [0]

            def step(ins):
                done[0] += 1
                ins.then_inc(window_step, 1)
                dve.wait_ge(window_step, done[0])

            step(nc.vector.memset(dst_f[:, :], -1.0))
            step(nc.vector.memset(dst_local[:, :], -1.0))
            step(nc.vector.memset(base_i[:, :], 0))
            step(nc.vector.memset(src_all[:, tiles:], 0))
            dve.wait_ge(consts_loaded, 16 * N_CONSTS)
            nc.vector.tensor_copy(ident_bf[:, :], ident[:, :]).then_inc(ident_cast, 1)
            dve.wait_ge(dst_loaded, 16)
            step(nc.vector.tensor_copy(dst_f[:, 0:tiles], dst_i[:, :]))
            step(nc.vector.tensor_reduce(
                least[:, :], dst_f[:, 0:tiles].rearrange("p (c t) -> p c t", t=TPC), AX_X, ALU.min))
            dve.wait_ge(least_moved, 1)
            step(nc.vector.tensor_reduce(
                least_t[0:per_group, :],
                xt_ps[0:per_group, 0:idx_groups * P].rearrange("p (g k) -> p g k", k=P), AX_X, ALU.min))
            dve.wait_ge(least_spread, 1)
            step(nc.vector.tensor_copy(
                base_f[:, :].rearrange("p (g k) -> p g k", k=per_group),
                dst_ps[:, 0:idx_groups * P].rearrange("p (g k) -> p g k", k=P)[:, :, 0:per_group]))
            step(nc.vector.tensor_copy(base_i[:, 0:chunks], base_f[:, :]))
            step(nc.vector.tensor_tensor(
                dst_local[:, 0:tiles].rearrange("p (c t) -> p c t", t=TPC),
                dst_f[:, 0:tiles].rearrange("p (c t) -> p c t", t=TPC),
                base_f[:, :].unsqueeze(2).broadcast_to([P, chunks, TPC]), ALU.subtract))
            step(nc.vector.tensor_reduce(top[:, :], dst_local[:, 0:tiles], AX_X, ALU.max))
            dve.wait_ge(top_moved, 1)
            step(nc.vector.tensor_reduce(top_one[:, 0:1], xt_ps[0:1, 0:P], AX_X, ALU.max))
            step(nc.vector.tensor_scalar(top_one[:, 1:2], top_one[:, 0:1], float(WIN), None, ALU.is_ge))
            nc.vector.tensor_copy(unfit[:, :], top_one[:, 1:2]).then_inc(unfit_known, 1)
            step(nc.vector.tensor_copy(dst_bf[:, :], dst_local[:, 0:tiles]))
            dve.wait_ge(src_loaded, 16)
            for j in range(SLOTS):
                nc.vector.tensor_copy(src_idx[:, j, :], src_all[:, j * TPC:(j + 1) * TPC]).then_inc(idx_copied, 1)
            dve.wait_ge(unfit_known, 1)

            def table_group(i, k, first):
                n = 2 * i + k
                dve.wait_ge(part_hi, n + 1)
                hi = parts[:, k, :, 0, :]
                mid = parts[:, k, :, 1, :]
                rest_k = rest[:, k, :].rearrange("p (b z) -> p b z", z=Z)
                if not first:
                    dve.wait_ge(part_lo, n - 1)
                nc.vector.tensor_tensor(rest_k, pre_ps[:, k, :].rearrange("p (b z) -> p b z", z=Z), hi,
                                        ALU.subtract).then_inc(part_rest, 1)
                dve.wait_ge(part_mid, n + 1)
                nc.vector.tensor_tensor(parts[:, k, :, 2, :], rest_k, mid, ALU.subtract).then_inc(part_lo, 1)

            for k in range(2):
                table_group(0, k, True)
            with dve.Fori(1, groups // 2) as i:
                for k in range(2):
                    table_group(i, k, False)

            def chunk(i, j, first):
                c = i * SLOTS + j
                dve.wait_ge(dst_spread, c + 1)
                if not first:
                    dve.wait_ge(z_done, c - SLOTS + 1)
                nc.vector.tensor_scalar(onehot_t[:, j, :], dst_ps[0:WIN, 0:CH], iota_col[0:WIN, 0:1], None,
                                        ALU.is_equal).then_inc(onehot_done, 1)
                dve.wait_ge(xt_done, c + 1)
                nc.vector.tensor_copy(src_idx[:, j, :], src_all[:, bass.ds((c + SLOTS) * TPC, TPC)])\
                    .then_inc(idx_copied, 1)
                if not (first and j == 0):
                    take_stats(c - 1, (j - 1) % SLOTS)

            def take_stats(c, j):
                dve.wait_ge(z_copied, c + 1)
                for h in range(2):
                    last = nc.vector.bn_stats(stats[:, bass.ds((2 * c + h) * 6, 6)],
                                              z_out[:, j, h * HALF:(h + 1) * HALF])
                last.then_inc(stats_done, 1)

            with dve.If(flag(dve) < 1):
                for j in range(SLOTS):
                    chunk(0, j, True)
                with dve.Fori(1, steps) as i:
                    for j in range(SLOTS):
                        chunk(i, j, False)
                take_stats(chunks - 1, SLOTS - 1)
                dve.wait_ge(stats_done, chunks)
            with dve.Else():
                def any_chunk(c, first):
                    if not first:
                        dve.wait_ge(any_stats, c)
                    nc.vector.tensor_copy(src_idx[:, 0, :], src_all[:, bass.ds(c * TPC, TPC)])\
                        .then_inc(window_step, 1)
                    dve.wait_ge(window_step, done[0] + 1 + c)
                    nc.vector.tensor_copy(dst_idx[:, :], dst_i[:, bass.ds(c * TPC, TPC)]).then_inc(any_idx, 1)
                    dve.wait_ge(any_turned, c + 1)
                    nc.vector.tensor_copy(x_dst_t[:, :], dst_ps[0:D, 0:CH]).then_inc(any_dst_copied, 1)
                    dve.wait_ge(any_z_copied, c + 1)
                    for h in range(2):
                        last = nc.vector.bn_stats(stats[:, bass.ds((2 * c + h) * 6, 6)],
                                                  z_out[:, 0, h * HALF:(h + 1) * HALF])
                    last.then_inc(any_stats, 1)

                any_chunk(0, True)
                with dve.Fori(1, chunks) as c:
                    any_chunk(c, False)
                dve.wait_ge(any_stats, chunks)

            nc.vector.bn_aggr(moments[:, :], stats[:, :]).then_inc(affine_step, 1)
            dve.wait_ge(affine_step, 1)
            nc.vector.tensor_scalar(small[:, 0:1], moments[:, 1:2], EPS, None, ALU.add).then_inc(affine_step, 1)
            nc.vector.memset(small[:, 1:2], -0.5).then_inc(affine_step, 1)
            dve.wait_ge(affine_step, 4)
            nc.vector.tensor_tensor(affine[:, 0:1], small[:, 2:3], bn1[:, 0:1], ALU.mult).then_inc(affine_step, 1)
            dve.wait_ge(affine_step, 5)
            nc.vector.tensor_tensor(small[:, 3:4], moments[:, 0:1], affine[:, 0:1], ALU.mult).then_inc(affine_step, 1)
            dve.wait_ge(affine_step, 6)
            nc.vector.tensor_tensor(affine[:, 1:2], bn1[:, 1:2], small[:, 3:4], ALU.subtract).then_inc(affine_step, 1)
            dve.wait_ge(affine_step, 7)

        @block.tensor
        def _(pe):
            pe.wait_ge(consts_loaded, 16 * N_CONSTS)
            pe.wait_ge(window_step, 6)
            for k in range(idx_groups):
                last = nc.tensor.transpose(xt_ps[0:per_group, k * P:(k + 1) * P],
                                           least[:, k * per_group:(k + 1) * per_group], ident[:, :])
            last.then_inc(least_moved, 1)
            pe.wait_ge(window_step, 7)
            for k in range(idx_groups):
                last = nc.tensor.matmul(dst_ps[:, k * P:k * P + per_group],
                                        least_t[0:per_group, k:k + 1].broadcast_to([per_group, P]),
                                        ident[0:per_group, 0:per_group], start=True, stop=True)
            last.then_inc(least_spread, 1)
            pe.wait_ge(window_step, 11)
            nc.tensor.transpose(xt_ps[0:1, 0:P], top[:, 0:1], ident[:, :]).then_inc(top_moved, 1)

            def table_group(i, k, first):
                n = 2 * i + k
                pe.wait_ge(x_group_loaded[k], 16 * (i + 1))
                if not first:
                    pe.wait_ge(part_rest, n - 1)
                for m in range(GROUP):
                    last = nc.tensor.matmul(pre_ps[:, k, m * Z:(m + 1) * Z], x_group[:, k, m * P:(m + 1) * P],
                                            w_dst[:, :], start=True, stop=True)
                last.then_inc(table_product, 1)

            for k in range(2):
                table_group(0, k, True)
            with pe.Fori(1, groups // 2) as i:
                for k in range(2):
                    table_group(i, k, False)
            pe.wait_ge(unfit_known, 1)
            pe.wait_ge(ident_cast, 1)
            pe.wait_ge(window_step, 14)

            def turn(to, rows):
                pe.sem_inc(turns_due, 1)
                for t in range(TPC):
                    last = nc.tensor.transpose(to[0:D, t * TILE:(t + 1) * TILE], rows[:, t * D:(t + 1) * D],
                                               ident[:, :])
                return last

            def prepare(i, j, first):
                c = i * SLOTS + j
                if not (first and j == 0):
                    pe.wait_ge(onehot_done, c)
                for t in range(TPC):
                    last = nc.tensor.matmul(dst_ps[0:WIN, t * TILE:(t + 1) * TILE],
                                            dst_bf[:, bass.ds(c * TPC + t, 1)].broadcast_to([P, WIN]),
                                            ident_bf[:, :], start=True, stop=True)
                last.then_inc(dst_spread, 1)
                pe.wait_ge(src_gathered[j], 16 * TPC * (i + 1))
                if not (first and j == 0):
                    pe.wait_ge(xt_copied, c)
                turn(xt_ps, x_src[:, j, :]).then_inc(xt_done, 1)

            def form_z(i, j, first):
                c = i * SLOTS + j
                pe.wait_ge(edges_loaded[j], 16 * (i + 1))
                pe.wait_ge(window_loaded[j], 16 * (i + 1))
                pe.wait_ge(onehot_done, c + 1)
                pe.wait_ge(xt_copied, c + 1)
                if not (first and j == 0):
                    pe.wait_ge(z_copied, c)
                for h in range(2):
                    cols = slice(h * HALF, (h + 1) * HALF)
                    nc.tensor.matmul(z_halves[:, h, :], w_both[:, :], feats[:, j, cols], start=True, stop=False)
                    for part in range(PARTS):
                        last = nc.tensor.matmul(z_halves[:, h, :], window[:, j, part * Z:(part + 1) * Z],
                                                onehot_t[:, j, cols], start=False, stop=part == PARTS - 1)
                last.then_inc(z_done, 1)

            with pe.If(flag(pe) < 1):
                prepare(0, 0, True)
                for j in range(1, SLOTS):
                    prepare(0, j, True)
                    form_z(0, j - 1, True)
                with pe.Fori(1, steps) as i:
                    for j in range(SLOTS):
                        prepare(i, j, False)
                        if j == 0:
                            form_z(i - 1, SLOTS - 1, False)
                        else:
                            form_z(i, j - 1, False)
                form_z(steps - 1, SLOTS - 1, False)
                pe.wait_ge(z_done, chunks)
            with pe.Else():
                with pe.Fori(0, chunks) as c:
                    pe.wait_ge(any_gathered, (c + 1) * 2 * TPC * 16)
                    turn(xt_ps, x_src[:, 0, :])
                    turn(dst_ps, x_dst[:, :]).then_inc(any_turned, 1)
                    pe.wait_ge(any_src_copied, c + 1)
                    pe.wait_ge(any_dst_copied, c + 1)
                    pe.wait_ge(any_edges, (c + 1) * 16)
                    for h in range(2):
                        cols = slice(h * HALF, (h + 1) * HALF)
                        nc.tensor.matmul(z_halves[:, h, :], w_both[:, :], feats[:, 0, cols], start=True, stop=False)
                        last = nc.tensor.matmul(z_halves[:, h, :], w_dst[:, :], x_dst_t[:, cols],
                                                start=False, stop=True)
                    last.then_inc(any_z, 1)
                pe.wait_ge(any_z, chunks)

        @block.scalar
        def _(act):
            def table_group(i, k, first):
                n = 2 * i + k
                act.wait_ge(table_product, n + 1)
                if not first:
                    act.wait_ge(table_stored[k], 16 * i)
                nc.scalar.activation(parts[:, k, :, 0, :], pre_ps[:, k, :].rearrange("p (b z) -> p b z", z=Z),
                                     ACT.Copy).then_inc(part_hi, 1)
                act.wait_ge(part_rest, n + 1)
                nc.scalar.activation(parts[:, k, :, 1, :], rest[:, k, :].rearrange("p (b z) -> p b z", z=Z),
                                     ACT.Copy).then_inc(part_mid, 1)
                act.wait_ge(part_lo, n + 1)
                act.dma_start(table[bass.ds(n * GROUP * P, GROUP * P), :].rearrange("(b p) f -> p b f", p=P),
                              parts[:, k, :, :, :].rearrange("p b s z -> p b (s z)")).then_inc(table_stored[k], 16)

            for k in range(2):
                table_group(0, k, True)
            with act.Fori(1, groups // 2) as i:
                for k in range(2):
                    table_group(i, k, False)
            act.wait_ge(unfit_known, 1)
            act.wait_ge(consts_loaded, 16 * N_CONSTS)

            def copy_features(i, j, first):
                c = i * SLOTS + j
                act.wait_ge(xt_done, c + 1)
                if not first:
                    act.wait_ge(z_done, c - SLOTS + 1)
                nc.scalar.activation(feats[0:D, j, :], xt_ps[0:D, 0:CH], ACT.Copy).then_inc(xt_copied, 1)

            def copy_z(i, j, first):
                c = i * SLOTS + j
                act.wait_ge(z_done, c + 1)
                if not first:
                    act.wait_ge(z_stored[j], 32 * i)
                    act.wait_ge(stats_done, c - SLOTS + 1)
                nc.scalar.activation(z_out[:, j, :].rearrange("p (h n) -> p h n", n=HALF), z_halves,
                                     ACT.Identity, bias=bias[:, 0:1]).then_inc(z_copied, 1)
                act.wait_ge(z_copied, c + 1)
                act.dma_start(z_gate[bass.ds(c * D, D), :], z_out[0:D, j, :]).then_inc(z_stored[j], 16)
                act.dma_start(z_core[bass.ds(c * D, D), :], z_out[D:P, j, :]).then_inc(z_stored[j], 16)

            with act.If(flag(act) < 1):
                copy_features(0, 0, True)
                for j in range(1, SLOTS):
                    copy_features(0, j, True)
                    copy_z(0, j - 1, True)
                with act.Fori(1, steps) as i:
                    for j in range(SLOTS):
                        copy_features(i, j, False)
                        if j == 0:
                            copy_z(i - 1, SLOTS - 1, False)
                        else:
                            copy_z(i, j - 1, False)
                copy_z(steps - 1, SLOTS - 1, False)
                for j in range(SLOTS):
                    act.wait_ge(z_stored[j], 32 * steps)
            with act.Else():
                def any_chunk(c, first):
                    act.wait_ge(any_turned, c + 1)
                    nc.scalar.activation(feats[0:D, 0, :], xt_ps[0:D, 0:CH], ACT.Copy).then_inc(any_src_copied, 1)
                    act.wait_ge(any_z, c + 1)
                    if not first:
                        act.wait_ge(any_stored, 32 * c)
                    nc.scalar.activation(z_out[:, 0, :].rearrange("p (h n) -> p h n", n=HALF), z_halves,
                                         ACT.Identity, bias=bias[:, 0:1]).then_inc(any_z_copied, 1)

                any_chunk(0, True)
                with act.Fori(1, chunks) as c:
                    any_chunk(c, False)
                act.wait_ge(any_z_copied, chunks)



def pass2(nc, a, sem, keep, sb_in, g):
    pairs, blocks, max_row = g["pairs"], g["blocks"], g["max_row"]
    z_gate, z_core = g["z_gate"], g["z_core"]
    ident, iota_row, dst_f, dst_local, base_i = g["ident"], g["iota_row"], g["dst_f"], g["dst_local"], g["base_i"]
    unfit, affine, sums = g["unfit"], g["affine"], g["sums"]
    body = 2 * PPH
    loops = pairs // body
    left = pairs - loops * body
    assert loops >= 1 and left <= PPH
    ptiles = 2 * TPC
    RING = 3
    HOTS = 4

    ctx = ExitStack()
    with ctx:
        def sb(name, shape, dt=F32):
            return sb_in(ctx, name, shape, dt)

        def ps(name, shape):
            return ctx.enter_context(nc.psum_tensor(name, shape, F32))

        gate = sb("gate", [P, 2, PPH * CH])
        core = sb("core", [P, 2, PPH * CH])
        soft = sb("soft", [P, 2, PPH * CH])
        message = sb("message", [P, RING, CH])
        onehot = sb("onehot", [P, HOTS, ptiles, WIN])
        gate_affine = sb("gate_affine", [P, 2])
        core_affine = sb("core_affine", [P, 2])
        any_local = sb("any_local", [P, TPC])
        turn_ps = ps("turn_ps", [P, RING, 2 * BANK])
        sum_ps = ps("sum_ps", [P, 2, BANK])

        affine_loaded = sem("affine_loaded")
        sums_zero = sem("sums_zero")
        gate_loaded = [[sem(f"gate_loaded{s}_{q}") for q in range(PPH // PIECE)] for s in range(2)]
        core_loaded = [[sem(f"core_loaded{s}_{q}") for q in range(PPH // PIECE)] for s in range(2)]
        sigmoid_done = sem("sigmoid_done")
        norms_due = sem("norms_due")
        normed = sem("normed")
        capped = sem("capped")
        exp_done = sem("exp_done")
        log_done = sem("log_done")
        softplus_done = sem("softplus_done")
        product_done = sem("product_done")
        turned = sem("turned")
        message_copied = sem("message_copied")
        onehot_made = sem("onehot_made")
        summed = sem("summed")
        sums_added = sem("sums_added")
        any_pair = sem("any_pair")
        any_local_made = sem("any_local_made")
        any_onehot = sem("any_onehot")
        any_summed = sem("any_summed")
        any_added = sem("any_added")

        def pieces(n):
            return [(q, min(PIECE, n - q * PIECE)) for q in range(-(-n // PIECE))]

        def spans(n):
            return [(lo, min(hi, n)) for lo, hi in ((0, 2 * PIECE), (2 * PIECE, PPH)) if lo < n]

        def place(i, k):
            return 2 * i + k // PPH, k % PPH

        block = ctx.enter_context(nc.Block())

        def flag(eng):
            return eng.value_load(unfit[0:1, 0:1], min_val=0, max_val=1)

        @block.sync
        def _(sp):
            for h in range(2):
                rows = slice(h * D, (h + 1) * D)
                sp.dma_start(gate_affine[rows, :], affine[0:D, :]).then_inc(affine_loaded, 16)
                sp.dma_start(core_affine[rows, :], affine[D:P, :]).then_inc(affine_loaded, 16)

            def load_half(i, s, n, first):
                half = 2 * i + s
                for q, m in pieces(n):
                    if not first:
                        sp.wait_ge(product_done, (half - 2) * PPH + (q + 1) * PIECE)
                    for buf, z, done in ((core, z_core, core_loaded), (gate, z_gate, gate_loaded)):
                        sp.dma_start(buf[:, s, q * PIECE * CH:(q * PIECE + m) * CH].rearrange("p (k n) -> p k n", n=CH),
                                     z[bass.ds((half * PPH + q * PIECE) * P, m * P), :]
                                     .rearrange("(k p) n -> p k n", p=P)).then_inc(done[s][q], 16)

            with sp.If(flag(sp) < 1):
                for s in range(2):
                    load_half(0, s, PPH, True)
                with sp.Fori(1, loops) as i:
                    for s in range(2):
                        load_half(i, s, PPH, False)
                if left:
                    load_half(loops, 0, left, False)
                sp.wait_ge(product_done, pairs)
            with sp.Else():
                def any_load(u, first):
                    if not first:
                        sp.wait_ge(any_pair, u)
                    sp.dma_start(gate[:, 0, 0:CH], z_gate[bass.ds(u * P, P), :]).then_inc(gate_loaded[0][0], 16)
                    sp.dma_start(core[:, 0, 0:CH], z_core[bass.ds(u * P, P), :]).then_inc(core_loaded[0][0], 16)

                any_load(0, True)
                with sp.Fori(1, pairs) as u:
                    any_load(u, False)
                sp.wait_ge(any_pair, pairs)
            sp.wait_ge(affine_loaded, 64)

        @block.gpsimd
        def _(pool):
            pool.wait_ge(affine_loaded, 64)

            def norm(s, first_pair, n):
                cols = slice(first_pair * CH, (first_pair + n) * CH)
                pool.sem_inc(norms_due, 1)
                nc.gpsimd.tensor_scalar(core[:, s, cols], core[:, s, cols], core_affine[:, 0:1],
                                        core_affine[:, 1:2], ALU.mult, ALU.add).then_inc(normed, 1)

            def cap(s, first_pair, n, number):
                cols = slice(first_pair * CH, (first_pair + n) * CH)
                pool.wait_ge(normed, number + 1)
                pool.sem_inc(norms_due, 1)
                nc.gpsimd.tensor_scalar(soft[:, s, cols], core[:, s, cols], SP_CAP, None, ALU.min)\
                    .then_inc(capped, 1)

            def norm_half(i, s, n, first):
                half = 2 * i + s
                for q, m in pieces(n):
                    pool.wait_ge(core_loaded[s][q], 16 * (i + 1))
                    norm(s, q * PIECE, m)
                    if not first:
                        pool.wait_ge(turned, (half - 2) * PPH + (q + 1) * PIECE)
                    cap(s, q * PIECE, m, half * (PPH // PIECE) + q)

            with pool.If(flag(pool) < 1):
                for s in range(2):
                    norm_half(0, s, PPH, True)
                with pool.Fori(1, loops) as i:
                    for s in range(2):
                        norm_half(i, s, PPH, False)
                if left:
                    norm_half(loops, 0, left, False)
            with pool.Else():
                with pool.Fori(0, pairs) as u:
                    pool.wait_ge(core_loaded[0][0], 16 * (u + 1))
                    norm(0, 0, 1)
                    cap(0, 0, 1, u)
            pool.wait_ge(sums_zero, 1)

        @block.scalar
        def _(act):
            act.wait_ge(affine_loaded, 64)

            def gates(s, lo, hi):
                cols = slice(lo * CH, hi * CH)
                nc.scalar.activation(gate[:, s, cols], gate[:, s, cols], ACT.Sigmoid,
                                     bias=gate_affine[:, 1:2], scale=gate_affine[:, 0:1]).then_inc(sigmoid_done, 1)

            def exps(s, lo, hi):
                cols = slice(lo * CH, hi * CH)
                nc.scalar.activation(soft[:, s, cols], soft[:, s, cols], ACT.Exp).then_inc(exp_done, 1)

            def logs(s, lo, hi, number):
                cols = slice(lo * CH, hi * CH)
                act.wait_ge(exp_done, number + 1)
                nc.scalar.activation(soft[:, s, cols], soft[:, s, cols], ACT.Ln, bias=1.0).then_inc(log_done, 1)

            def copy_message(i, k, first):
                u = i * body + k
                act.wait_ge(turned, u + 1)
                if not first:
                    act.wait_ge(summed, u - RING + 1)
                nc.scalar.activation(message[:, k % RING, :], turn_ps[:, k % RING, 0:CH], ACT.Copy)\
                    .then_inc(message_copied, 1)

            def half(i, s, n, first):
                number = 2 * i + s
                copies = iter([] if first and s == 0 else range((s - 1) * PPH, s * PPH))

                def copy_one():
                    for k in copies:
                        copy_message(i, k, first and k < RING)
                        break

                for lo, hi in spans(n):
                    for q in range(lo // PIECE, -(-hi // PIECE)):
                        act.wait_ge(gate_loaded[s][q], 16 * (i + 1))
                    gates(s, lo, hi)
                    copy_one()
                nc.scalar.preload_act_table_set(EXP_LN_SET)
                for lo, hi in spans(n):
                    act.wait_ge(capped, number * (PPH // PIECE) + -(-hi // PIECE))
                    exps(s, lo, hi)
                    copy_one()
                for at, (lo, hi) in enumerate(spans(n)):
                    logs(s, lo, hi, 2 * number + at)
                    copy_one()
                for k in copies:
                    copy_message(i, k, first and k < RING)

            with act.If(flag(act) < 1):
                for s in range(2):
                    half(0, s, PPH, True)
                with act.Fori(1, loops) as i:
                    for s in range(2):
                        half(i, s, PPH, False)
                if left:
                    half(loops, 0, left, False)
                for k in range(left) if left else range(-PPH, 0):
                    copy_message(loops, k, False)
                act.wait_ge(log_done, 4 * loops + len(spans(left)))
            with act.Else():
                with act.Fori(0, pairs) as u:
                    act.wait_ge(gate_loaded[0][0], 16 * (u + 1))
                    gates(0, 0, 1)
                    nc.scalar.preload_act_table_set(EXP_LN_SET)
                    act.wait_ge(capped, u + 1)
                    exps(0, 0, 1)
                    logs(0, 0, 1, u)
                act.wait_ge(log_done, pairs)

        @block.vector
        def _(dve):
            nc.vector.memset(sums[:, :], 0.0).then_inc(sums_zero, 1)
            dve.wait_ge(sums_zero, 1)

            iota_many = iota_row[:, 0:WIN].unsqueeze(1).broadcast_to([P, ptiles, WIN])

            def mark(u, k, first):
                if not first:
                    dve.wait_ge(summed, u - HOTS + 1)
                nc.vector.tensor_tensor(
                    onehot[:, k % HOTS, :, :], iota_many,
                    dst_local[:, bass.ds(u * ptiles, ptiles)].unsqueeze(2).broadcast_to([P, ptiles, WIN]),
                    ALU.is_equal).then_inc(onehot_made, 1)

            def combine(s, p, u, span):
                cols = slice(p * CH, (p + 1) * CH)
                dve.wait_ge(log_done, span + 1)
                nc.vector.tensor_tensor(soft[:, s, cols], soft[:, s, cols], core[:, s, cols], ALU.max)\
                    .then_inc(softplus_done, 1)
                dve.wait_ge(softplus_done, u + 1)
                dve.wait_ge(sigmoid_done, span + 1)
                nc.vector.tensor_tensor(soft[:, s, cols], soft[:, s, cols], gate[:, s, cols], ALU.mult)\
                    .then_inc(product_done, 1)

            def window_starts(u):
                return [dve.value_load(base_i[0:1, bass.ds(2 * u + h, 1)], min_val=0, max_val=max_row)
                        for h in range(2)]

            def add_sums(u, r, starts, first):
                dve.wait_ge(summed, u + 1)
                for h, node in enumerate(starts):
                    rows = slice(h * D, (h + 1) * D)
                    if not first:
                        dve.wait_ge(sums_added, 2 * u + h - 1)
                    nc.vector.tensor_tensor(sums[rows, bass.ds(node, WIN)], sums[rows, bass.ds(node, WIN)],
                                            sum_ps[rows, r, 0:WIN], ALU.add).then_inc(sums_added, 1)

            def pair(i, k, first):
                u = i * body + k
                half, p = place(i, k)
                starts = None if first and k < 3 else window_starts(u - 3)
                combine(k // PPH, p, u, 2 * half + p // (2 * PIECE))
                mark(u, k, first and k < HOTS)
                if starts:
                    add_sums(u - 3, (k - 3) % 2, starts, first and k == 3)

            with dve.If(flag(dve) < 1):
                for k in range(body):
                    pair(0, k, True)
                with dve.Fori(1, loops) as i:
                    for k in range(body):
                        pair(i, k, False)
                for k in range(left):
                    pair(loops, k, False)
                for u in range(pairs - 3, pairs):
                    add_sums(u, u % 2, window_starts(u), False)
                dve.wait_ge(sums_added, 2 * pairs)
            with dve.Else():
                by_block = onehot[:, 0, :, :].rearrange("p t w -> p (t w)").rearrange("p (t w) -> p t w", w=P)

                def any_window(u, h, w):
                    n = (2 * u + h) * blocks + w
                    rows = slice(h * D, (h + 1) * D)
                    dve.wait_ge(any_local_made, n + 2 * u + h + 1)
                    nc.vector.tensor_tensor(
                        by_block, iota_row[:, :].unsqueeze(1).broadcast_to([P, TPC, P]),
                        any_local[:, :].unsqueeze(2).broadcast_to([P, TPC, P]), ALU.is_equal)\
                        .then_inc(any_onehot, 1)
                    dve.wait_ge(any_onehot, n + 1)
                    nc.vector.tensor_scalar(any_local[:, :], any_local[:, :], float(P), None, ALU.subtract)\
                        .then_inc(any_local_made, 1)
                    dve.wait_ge(any_summed, n + 1)
                    nc.vector.tensor_tensor(sums[rows, bass.ds(w * P, P)], sums[rows, bass.ds(w * P, P)],
                                            sum_ps[rows, 0, 0:P], ALU.add).then_inc(any_added, 1)

                with dve.Fori(0, pairs) as u:
                    combine(0, 0, u, u)
                    dve.wait_ge(turned, u + 1)
                    nc.vector.tensor_copy(message[:, 0, :], turn_ps[:, 0, 0:CH]).then_inc(message_copied, 1)
                    for h in range(2):
                        if h:
                            dve.wait_ge(any_local_made, (2 * u + h) * (blocks + 1))
                        nc.vector.tensor_copy(any_local[:, :], dst_f[:, bass.ds((2 * u + h) * TPC, TPC)])\
                            .then_inc(any_local_made, 1)
                        with dve.Fori(0, blocks) as w:
                            any_window(u, h, w)
                    dve.wait_ge(any_local_made, (2 * u + 2) * (blocks + 1))
                    dve.wait_ge(any_added, (2 * u + 2) * blocks)
                    nc.vector.memset(any_local[:, :], 0.0).then_inc(any_pair, 1)
                    dve.wait_ge(any_pair, u + 1)

        @block.tensor
        def _(pe):
            def turn(s, p, r):
                for t in range(TPC):
                    at = p * CH + t * TILE
                    last = nc.tensor.transpose(turn_ps[:, r, t * P:(t + 1) * P], soft[:, s, at:at + TILE],
                                               ident[:, :])
                last.then_inc(turned, 1)

            def turn_pair(i, k, first):
                pe.wait_ge(product_done, i * body + k + 1)
                if not first:
                    pe.wait_ge(message_copied, i * body + k - RING + 1)
                turn(k // PPH, k % PPH, k % RING)

            def sum_pair(i, k, first):
                u = i * body + k
                pe.wait_ge(message_copied, u + 1)
                pe.wait_ge(onehot_made, u + 1)
                if not first:
                    pe.wait_ge(sums_added, 2 * u - 2)
                for h in range(2):
                    for t in range(TPC):
                        last = nc.tensor.matmul(sum_ps[h * D:(h + 1) * D, k % 2, 0:WIN],
                                                message[:, k % RING, t * P + h * D:t * P + (h + 1) * D],
                                                onehot[:, k % HOTS, h * TPC + t, :],
                                                start=t == 0, stop=t == TPC - 1)
                last.then_inc(summed, 1)

            def pair(i, k, first):
                if not (first and k < 2):
                    sum_pair(i, k - 2, first and k < 4)
                turn_pair(i, k, first and k < RING)

            with pe.If(flag(pe) < 1):
                for k in range(body):
                    pair(0, k, True)
                with pe.Fori(1, loops) as i:
                    for k in range(body):
                        pair(i, k, False)
                for k in range(left):
                    pair(loops, k, False)
                for k in range(left - 2, left):
                    sum_pair(loops, k, False)
                pe.wait_ge(summed, pairs)
            with pe.Else():
                with pe.Fori(0, pairs) as u:
                    pe.wait_ge(product_done, u + 1)
                    turn(0, 0, 0)
                    for h in range(2):
                        with pe.Fori(0, blocks) as w:
                            pe.wait_ge(message_copied, u + 1)
                            pe.wait_ge(any_onehot, (2 * u + h) * blocks + w + 1)
                            for t in range(TPC):
                                last = nc.tensor.matmul(sum_ps[h * D:(h + 1) * D, 0, 0:P],
                                                        message[:, 0, t * P + h * D:t * P + (h + 1) * D],
                                                        onehot[:, 0, 2 * t:2 * t + 2, :].rearrange("p a w -> p (a w)"),
                                                        start=t == 0, stop=t == TPC - 1)
                            last.then_inc(any_summed, 1)
                pe.wait_ge(any_summed, 2 * pairs * blocks)


def nodes(nc, a, out, sem, keep, sb_in, g):
    n_nodes = a["x"].shape[0]
    half = n_nodes // 2
    sums = g["sums"]
    pieces = [(at, min(BANK, half - at)) for at in range(0, half, BANK)]
    n = len(pieces)

    ctx = ExitStack()
    with ctx:
        def sb(name, shape, dt=F32):
            return sb_in(ctx, name, shape, dt)

        def ps(name, shape):
            return ctx.enter_context(nc.psum_tensor(name, shape, F32))

        x_half = sb("x_half", [P, half])
        update = sb("update", [P, half])
        work = sb("work", [P, half])
        total = sb("total", [P, half])
        fold = sb("fold", [P, D])
        fold_wide = sb("fold_wide", [P, P])
        channel_mean = sb("channel_mean", [P, P])
        bn2 = sb("bn2", [P, 2])
        stats2 = sb("stats2", [P, 6 * n])
        moments2 = sb("moments2", [P, 2])
        small2 = sb("small2", [P, 6])
        eps_col = sb("eps_col", [P, 1])
        node_ps = ps("node_ps", [P, 2, BANK])
        mean_ps = ps("mean_ps", [P, 2, BANK])
        var_ps = ps("var_ps", [P, 2, BANK])
        both_ps = ps("both_ps", [P, BANK])

        loaded = sem("nodes_loaded")
        x_loaded = sem("x_loaded")
        eps_set = sem("eps_set")
        folded = sem("folded")
        fold_copied = sem("fold_copied")
        stats2_step = sem("stats2_step")
        both_added = sem("both_added")
        power_done = sem("power_done")
        offset_step = sem("offset_step")
        scaled = sem("scaled")
        capped = sem("node_capped")
        exp_done = sem("node_exp_done")
        log_done = sem("node_log_done")
        softplus_done = sem("node_softplus_done")
        total_done = sem("total_done")
        mean_done = sem("mean_done")
        centered = sem("centered")
        squared = sem("squared")
        var_done = sem("var_done")
        var_log = sem("var_log")
        deviation_done = sem("deviation_done")
        result_done = sem("result_done")
        out_stored = sem("out_stored")
        block = ctx.enter_context(nc.Block())

        def cols(k):
            at, width = pieces[k]
            return slice(at, at + width)

        def width(k):
            return slice(0, pieces[k][1])

        @block.sync
        def _(sp):
            sp.dma_start(fold[:, :], a["fold"]).then_inc(loaded, 16)
            sp.dma_start(x_half[:, :], a["x_halves"]).then_inc(x_loaded, 16)
            for k in range(n):
                sp.wait_ge(result_done, k + 1)
                sp.dma_start(out[:, cols(k)], total[:, cols(k)]).then_inc(out_stored, 16)
            sp.wait_ge(out_stored, 16 * n)

        @block.gpsimd
        def _(pool):
            pool.wait_ge(stats2_step, n + 8)
            nc.gpsimd.tensor_tensor(small2[:, 4:5], small2[:, 2:3], small2[:, 3:4], ALU.pow).then_inc(power_done, 1)
            for k in range(n):
                pool.wait_ge(softplus_done, k + 1)
                nc.gpsimd.tensor_tensor(total[:, cols(k)], work[:, cols(k)], x_half[:, cols(k)], ALU.add)\
                    .then_inc(total_done, 1)

        @block.scalar
        def _(act):
            for h in range(2):
                act.dma_start(bn2[h * D:(h + 1) * D, 0:1], a["gamma2"]).then_inc(loaded, 16)
                act.dma_start(bn2[h * D:(h + 1) * D, 1:2], a["beta2"]).then_inc(loaded, 16)
            act.dma_start(fold_wide[:, :], a["fold_wide"]).then_inc(loaded, 16)
            act.dma_start(channel_mean[:, :], a["channel_mean"]).then_inc(loaded, 16)
            for k in range(n):
                act.wait_ge(folded, k + 1)
                nc.scalar.activation(update[:, cols(k)], node_ps[:, k % 2, width(k)], ACT.Copy).then_inc(fold_copied, 1)
            nc.scalar.preload_act_table_set(EXP_LN_SET)
            act.wait_ge(eps_set, 1)

            def softplus(k):
                act.wait_ge(capped, k + 1)
                nc.scalar.activation(work[:, cols(k)], work[:, cols(k)], ACT.Exp).then_inc(exp_done, 1)
                act.wait_ge(exp_done, k + 1)
                nc.scalar.activation(work[:, cols(k)], work[:, cols(k)], ACT.Ln, bias=1.0).then_inc(log_done, 1)

            def square(k):
                act.wait_ge(centered, k + 1)
                nc.scalar.activation(work[:, cols(k)], total[:, cols(k)], ACT.Square).then_inc(squared, 1)

            def deviation(k):
                act.wait_ge(var_done, k + 1)
                nc.scalar.activation(work[:, cols(k)], var_ps[:, k % 2, width(k)], ACT.Ln,
                                     bias=eps_col[:, 0:1]).then_inc(var_log, 1)
                act.wait_ge(var_log, k + 1)
                nc.scalar.activation(work[:, cols(k)], work[:, cols(k)], ACT.Exp, scale=-0.5)\
                    .then_inc(deviation_done, 1)

            for k in range(n + 4):
                if k < n:
                    softplus(k)
                if 2 <= k < n + 2:
                    square(k - 2)
                if 4 <= k:
                    deviation(k - 4)

        @block.tensor
        def _(pe):
            pe.wait_ge(loaded, 16 * 7)
            for k in range(n):
                if k >= 2:
                    pe.wait_ge(fold_copied, k - 1)
                for h in range(2):
                    at, w = pieces[k]
                    last = nc.tensor.matmul(node_ps[h * D:(h + 1) * D, k % 2, 0:w], fold[:, :],
                                            sums[:, h * half + at:h * half + at + w], start=True, stop=True)
                last.then_inc(folded, 1)
            pe.wait_ge(stats2_step, n + 1)
            nc.tensor.matmul(both_ps[:, 0:2], fold_wide[:, :], moments2[:, :], start=True, stop=True)\
                .then_inc(both_added, 1)
            for k in range(n + 1):
                if k < n:
                    pe.wait_ge(total_done, k + 1)
                    if k >= 2:
                        pe.wait_ge(centered, k - 1)
                    nc.tensor.matmul(mean_ps[:, k % 2, width(k)], channel_mean[:, :], total[:, cols(k)],
                                     start=True, stop=True).then_inc(mean_done, 1)
                if k >= 1:
                    pe.wait_ge(squared, k)
                    if k >= 3:
                        pe.wait_ge(var_log, k - 2)
                    nc.tensor.matmul(var_ps[:, (k - 1) % 2, width(k - 1)], channel_mean[:, :],
                                     work[:, cols(k - 1)], start=True, stop=True).then_inc(var_done, 1)

        @block.vector
        def _(dve):
            nc.vector.memset(eps_col[:, :], EPS).then_inc(eps_set, 1)
            for k in range(n):
                dve.wait_ge(fold_copied, k + 1)
                nc.vector.bn_stats(stats2[:, 6 * k:6 * (k + 1)], update[:, cols(k)]).then_inc(stats2_step, 1)
            done = [n]

            def step(ins):
                done[0] += 1
                ins.then_inc(stats2_step, 1)
                dve.wait_ge(stats2_step, done[0])

            dve.wait_ge(stats2_step, n)
            step(nc.vector.bn_aggr(moments2[:, :], stats2[:, :]))
            dve.wait_ge(both_added, 1)
            step(nc.vector.tensor_scalar(small2[:, 0:2], both_ps[:, 0:2], 0.5, None, ALU.mult))
            step(nc.vector.tensor_tensor(small2[:, 2:3], moments2[:, 0:1], small2[:, 0:1], ALU.subtract))
            step(nc.vector.tensor_tensor(small2[:, 2:3], small2[:, 2:3], small2[:, 2:3], ALU.mult))
            step(nc.vector.tensor_tensor(small2[:, 2:3], small2[:, 2:3], small2[:, 1:2], ALU.add))
            step(nc.vector.tensor_scalar(small2[:, 2:3], small2[:, 2:3], EPS, None, ALU.add))
            step(nc.vector.memset(small2[:, 3:4], -0.5))
            dve.wait_ge(loaded, 16 * 7)
            step(nc.vector.tensor_copy(small2[:, 5:6], bn2[:, 1:2]))
            dve.wait_ge(power_done, 1)
            step(nc.vector.tensor_tensor(small2[:, 4:5], small2[:, 4:5], bn2[:, 0:1], ALU.mult))
            step(nc.vector.tensor_tensor(small2[:, 3:4], small2[:, 0:1], small2[:, 4:5], ALU.mult))
            step(nc.vector.tensor_tensor(small2[:, 5:6], small2[:, 5:6], small2[:, 3:4], ALU.subtract))
            scale, offset = small2[:, 4:5], small2[:, 5:6]
            dve.wait_ge(x_loaded, 16)

            def node_update(k):
                nc.vector.scalar_tensor_tensor(out=update[:, cols(k)], in0=update[:, cols(k)], scalar=scale,
                                               in1=x_half[:, cols(k)], op0=ALU.mult, op1=ALU.add).then_inc(scaled, 1)
                dve.wait_ge(scaled, k + 1)
                nc.vector.tensor_scalar(work[:, cols(k)], update[:, cols(k)], offset, SP_CAP, ALU.add, ALU.min)\
                    .then_inc(capped, 1)

            def softplus(k):
                dve.wait_ge(log_done, k + 1)
                nc.vector.scalar_tensor_tensor(out=work[:, cols(k)], in0=update[:, cols(k)], scalar=offset,
                                               in1=work[:, cols(k)], op0=ALU.add, op1=ALU.max)\
                    .then_inc(softplus_done, 1)

            def center(k):
                dve.wait_ge(mean_done, k + 1)
                nc.vector.tensor_tensor(total[:, cols(k)], total[:, cols(k)], mean_ps[:, k % 2, width(k)],
                                        ALU.subtract).then_inc(centered, 1)

            def result(k):
                dve.wait_ge(deviation_done, k + 1)
                nc.vector.tensor_tensor(total[:, cols(k)], total[:, cols(k)], work[:, cols(k)], ALU.mult)\
                    .then_inc(result_done, 1)

            for k in range(n + 5):
                if k < n:
                    node_update(k)
                if 1 <= k < n + 1:
                    softplus(k - 1)
                if 2 <= k < n + 2:
                    center(k - 2)
                if 5 <= k:
                    result(k - 5)
            dve.wait_ge(result_done, n)


def kernel(**inputs):
    import concourse.bacc as bacc
    from concourse.bass_utils import run_bass_kernel_spmd

    x = np.asarray(inputs["x"])
    src = np.asarray(inputs["src"])
    dst = np.asarray(inputs["dst"])
    edges = np.asarray(inputs["edge_attr_64"])
    n_nodes, n_edges = x.shape[0], src.shape[0]
    chunks, blocks, groups, pairs = sizes(n_nodes, n_edges)

    x_t = np.zeros((D, groups * GROUP * P), x.dtype)
    x_t[:, :n_nodes] = x.T
    iota = np.arange(P, dtype=np.float32)
    arrays = {
        "x": x,
        "x_groups": np.ascontiguousarray(x_t.reshape(D, groups, GROUP * P).transpose(1, 0, 2)).reshape(-1, GROUP * P),
        "src_cols": np.ascontiguousarray(src.reshape(-1, TILE).T),
        "dst_cols": np.ascontiguousarray(dst.reshape(-1, TILE).T),
        "edge_chunks": np.ascontiguousarray(edges.reshape(chunks, CH, D).transpose(0, 2, 1)).reshape(-1, CH),
        "w": np.asarray(inputs["L0_gnn_W"]),
        "b": np.asarray(inputs["L0_gnn_b"]).reshape(Z, 1),
        "gamma1": np.asarray(inputs["L0_gnn_bn1_gamma"]).reshape(Z, 1),
        "beta1": np.asarray(inputs["L0_gnn_bn1_beta"]).reshape(Z, 1),
        "gamma2": np.asarray(inputs["L0_gnn_bn2_gamma"]).reshape(D, 1),
        "beta2": np.asarray(inputs["L0_gnn_bn2_beta"]).reshape(D, 1),
        "ident": np.eye(P, dtype=np.float32),
        "iota_row": np.tile(iota, (P, 1)),
        "iota_col": iota.reshape(P, 1).copy(),
        "fold": np.tile(np.eye(D, dtype=np.float32), (2, 1)),
        "fold_wide": np.tile(np.eye(D, dtype=np.float32), (2, 2)),
        "channel_mean": np.kron(np.eye(2, dtype=np.float32), np.full((D, D), 1.0 / D, np.float32)),
        "x_halves": np.ascontiguousarray(x.reshape(2, n_nodes // 2, D).transpose(0, 2, 1)).reshape(P, -1),
    }
    nc = bacc.Bacc("TRN2", target_bir_lowering=False, num_devices=1)
    aps = {name: nc.dram_tensor(f"in_{name}", v.shape, mybir.dt.from_np(v.dtype), kind="ExternalInput").ap()
           for name, v in arrays.items()}
    out = nc.dram_tensor("out", (P, n_nodes // 2), F32, kind="ExternalOutput").ap()
    build_program(nc, aps, out)
    got = run_bass_kernel_spmd(nc, [{f"in_{name}": v for name, v in arrays.items()}], core_ids=[0])
    return np.asarray(got.results[0]["out"]).reshape(2, D, n_nodes // 2).transpose(0, 2, 1).reshape(n_nodes, D)
```

```python
from contextlib import ExitStack

import numpy as np

import concourse.bass as bass
from concourse import mybir

F32 = mybir.dt.float32
BF16 = mybir.dt.bfloat16
I32 = mybir.dt.int32
ALU = mybir.AluOpType
ACT = mybir.ActivationFunctionType
AX_X = mybir.AxisListType.X

P = 128
D = 64
Z = 2 * D
TILE = 128
TPC = 5
CH = TPC * TILE
HALF = CH // 2
BANK = 512
SLOTS = 5
WIN = 64
AHEAD = 2 * SLOTS
PARTS = 3
GROUP = 4
TSLOTS = 5
PPH = 6
PIECE = 2
EPS = 1e-5
EXP_LN_SET = "natural_log_exp_and_others"
SP_CAP = 30.0


def sizes(n_nodes, n_edges):
    chunks = n_edges // CH
    assert chunks * CH == n_edges and chunks % SLOTS == 0 and chunks // SLOTS % 2 == 1
    blocks = -(-n_nodes // P)
    groups = -(-(n_nodes - 1 + WIN) // (GROUP * P))
    groups += -groups % TSLOTS
    pairs = -(-chunks // 2)
    return chunks, blocks, groups, pairs


class Whole:
    pass


def build_program(nc, a, out):
    n_nodes = a["x"].shape[0]
    n_edges = a["src_cols"].shape[1] * TILE
    chunks, blocks, groups, pairs = sizes(n_nodes, n_edges)
    tiles = chunks * TPC
    pair_tiles = 2 * pairs * TPC
    steps = chunks // SLOTS
    max_row = n_nodes - 1
    node_cols = max(blocks * P, n_nodes + WIN)
    idx_groups = -(-chunks // P)
    assert chunks % idx_groups == 0 and n_nodes % 2 == 0
    per_group = chunks // idx_groups

    table = nc.dram_tensor("dst_table", (groups * GROUP * P, PARTS * Z), BF16, kind="Internal").ap()
    z_gate = nc.dram_tensor("z_gate", (2 * pairs * D, CH), F32, kind="Internal").ap()
    z_core = nc.dram_tensor("z_core", (2 * pairs * D, CH), F32, kind="Internal").ap()

    keep = ExitStack()
    with keep:
        def sb_in(ctx, name, shape, dt=F32):
            return ctx.enter_context(nc.sbuf_tensor(name, shape, dt))

        def sem(name):
            return keep.enter_context(nc.semaphore(name))

        ident = sb_in(keep, "ident", [P, P])
        iota_row = sb_in(keep, "iota_row", [P, P])
        dst_f = sb_in(keep, "dst_f", [P, pair_tiles])
        dst_local = sb_in(keep, "dst_local", [P, pair_tiles])
        base_i = sb_in(keep, "base_i", [P, 2 * pairs], I32)
        unfit = sb_in(keep, "unfit", [1, 1], I32)
        gate_affine = sb_in(keep, "gate_affine", [P, 2])
        core_affine = sb_in(keep, "core_affine", [P, 2])
        fold = sb_in(keep, "fold", [P, D])
        fold_wide = sb_in(keep, "fold_wide", [P, P])
        channel_mean = sb_in(keep, "channel_mean", [P, P])
        bn2 = sb_in(keep, "bn2", [P, 2])

        whole = Whole()
        whole.chunks, whole.blocks, whole.groups, whole.pairs, whole.tiles = chunks, blocks, groups, pairs, tiles
        whole.pair_tiles, whole.steps, whole.max_row = pair_tiles, steps, max_row
        whole.idx_groups, whole.per_group = idx_groups, per_group
        whole.table, whole.z_gate, whole.z_core, whole.ident, whole.iota_row = table, z_gate, z_core, ident, iota_row
        whole.dst_f, whole.dst_local, whole.base_i, whole.unfit = dst_f, dst_local, base_i, unfit
        whole.gate_affine, whole.core_affine = gate_affine, core_affine
        whole.fold, whole.fold_wide, whole.channel_mean, whole.bn2 = fold, fold_wide, channel_mean, bn2
        pass1(nc, a, sem, sb_in, whole)
        whole.sums = sb_in(keep, "sums", [P, node_cols])
        pass2(nc, sem, sb_in, whole)
        nodes(nc, a, out, sem, sb_in, whole)
    return nc


def pass1(nc, a, sem, sb_in, whole):
    chunks, groups, pairs, tiles, steps = whole.chunks, whole.groups, whole.pairs, whole.tiles, whole.steps
    pair_tiles, max_row, idx_groups, per_group = whole.pair_tiles, whole.max_row, whole.idx_groups, whole.per_group
    table, z_gate, z_core = whole.table, whole.z_gate, whole.z_core
    ident, iota_row, dst_f, dst_local, base_i = whole.ident, whole.iota_row, whole.dst_f, whole.dst_local, whole.base_i
    unfit, gate_affine, core_affine = whole.unfit, whole.gate_affine, whole.core_affine
    fold, fold_wide, channel_mean, bn2 = whole.fold, whole.fold_wide, whole.channel_mean, whole.bn2

    ctx = ExitStack()
    with ctx:
        def sb(name, shape, dt=F32):
            return sb_in(ctx, name, shape, dt)

        def ps(name, shape):
            return ctx.enter_context(nc.psum_tensor(name, shape, F32))

        ident_bf = sb("ident_bf", [P, P], BF16)
        iota_col = sb("iota_col", [P, 1])
        w_both = sb("w_both", [P, Z])
        w_dst = sb("w_dst", [D, Z])
        bias = sb("bias", [P, 1])
        bn1 = sb("bn1", [P, 2])
        src_all = sb("src_all", [P, tiles + AHEAD * TPC], I32)
        dst_i = sb("dst_i", [P, tiles], I32)
        dst_bf = sb("dst_bf", [P, tiles], BF16)
        least = sb("least", [P, chunks])
        least_t = sb("least_t", [P, idx_groups])
        base_f = sb("base_f", [P, chunks])
        top = sb("top", [P, 1])
        top_one = sb("top_one", [1, 4])
        x_group = sb("x_group", [D, TSLOTS, GROUP * P])
        rest = sb("rest", [P, TSLOTS, GROUP * Z])
        parts = sb("parts", [P, TSLOTS, GROUP, PARTS, Z], BF16)
        src_idx = sb("src_idx", [P, AHEAD, TPC], I32)
        dst_idx = sb("dst_idx", [P, TPC], I32)
        x_src = sb("x_src", [P, AHEAD, TPC * D])
        x_dst = sb("x_dst", [P, TPC * D])
        feats = sb("feats", [P, SLOTS, CH])
        x_dst_t = sb("x_dst_t", [D, CH])
        window = sb("window", [WIN, SLOTS, PARTS * Z], BF16)
        onehot_t = sb("onehot_t", [WIN, SLOTS, CH], BF16)
        z_out = sb("z_out", [P, SLOTS, CH])
        to_gate = sb("to_gate", [P, P])
        to_core = sb("to_core", [P, P])
        stats = sb("stats", [P, 12])
        chunk_moments = sb("chunk_moments", [P, chunks, 2])
        chunk_now = sb("chunk_now", [P, 2])
        mean_stats = sb("mean_stats", [P, 6 * SLOTS])
        moments = sb("moments", [P, 2])
        affine = sb("affine", [P, 2])
        small = sb("small", [P, 4])
        zero = sb("zero", [D, CH])

        xt_ps = ps("xt_ps", [P, 2 * BANK])
        dst_ps = ps("dst_ps", [P, 2 * BANK])
        z_ps = ps("z_ps", [P, 2 * BANK])
        pre_ps = ps("pre_ps", [P, 2, BANK])
        product_ps = [pre_ps[:, 0, :], pre_ps[:, 1, :], z_ps[:, 0:BANK], z_ps[:, BANK:], xt_ps[:, BANK:]]
        z_halves = z_ps[:, :].rearrange("p (h n) -> p h n", n=BANK)[:, :, 0:HALF]

        consts_loaded = sem("consts_loaded")
        src_loaded = sem("src_loaded")
        late_consts_loaded = sem("late_consts_loaded")
        dst_loaded = sem("dst_loaded")
        zero_made = sem("zero_made")
        pad_stored = sem("pad_stored")
        x_group_loaded = [sem(f"x_group_loaded{k}") for k in range(TSLOTS)]
        window_step = sem("window_step")
        least_moved = sem("least_moved")
        least_spread = sem("least_spread")
        top_moved = sem("top_moved")
        unfit_known = sem("unfit_known")
        table_product = sem("table_product")
        part_hi = sem("part_hi")
        part_rest = sem("part_rest")
        part_mid = sem("part_mid")
        part_lo = sem("part_lo")
        table_stored = [sem(f"table_stored{k}") for k in range(TSLOTS)]
        ident_cast = sem("ident_cast")
        idx_copied = sem("idx_copied")
        src_gathered = [sem(f"src_gathered{j}") for j in range(AHEAD)]
        gathers_due = sem("gathers_due")
        turns_due = sem("turns_due")
        dst_spread = sem("dst_spread")
        onehot_done = sem("onehot_done")
        xt_done = sem("xt_done")
        xt_copied = sem("xt_copied")
        edges_loaded = [sem(f"edges_loaded{j}") for j in range(SLOTS)]
        window_loaded = [sem(f"window_loaded{j}") for j in range(SLOTS)]
        z_done = sem("z_done")
        z_copied = sem("z_copied")
        halves_done = sem("halves_done")
        moments_due = sem("moments_due")
        chunk_aggregated = sem("chunk_aggregated")
        stats_done = sem("stats_done")
        z_stored = [sem(f"z_stored{j}") for j in range(SLOTS)]
        affine_step = sem("affine_step")
        affine_moved = sem("affine_moved")
        any_idx = sem("any_idx")
        any_gathered = sem("any_gathered")
        any_turned = sem("any_turned")
        any_src_copied = sem("any_src_copied")
        any_dst_copied = sem("any_dst_copied")
        any_edges = sem("any_edges")
        any_z = sem("any_z")
        any_z_copied = sem("any_z_copied")
        any_stats = sem("any_stats")
        any_stored = sem("any_stored")

        block = ctx.enter_context(nc.Block())
        N_CONSTS = 9
        N_LATE = 9

        def flag(eng):
            return eng.value_load(unfit[0:1, 0:1], min_val=0, max_val=1)

        @block.sync
        def _(sp):
            sp.dma_start(dst_i[:, :], a["dst_cols"]).then_inc(dst_loaded, 16)
            sp.dma_start(ident[:, :], a["ident"]).then_inc(consts_loaded, 16)
            sp.dma_start(iota_row[:, :], a["iota_row"]).then_inc(consts_loaded, 16)
            sp.dma_start(iota_col[:, :], a["iota_col"]).then_inc(consts_loaded, 16)
            sp.dma_start(w_both[0:D, :], a["w"][0:D, :]).then_inc(consts_loaded, 16)
            sp.dma_start(w_both[D:P, :], a["w"][2 * D:3 * D, :]).then_inc(consts_loaded, 16)
            sp.dma_start(w_dst[:, :], a["w"][D:2 * D, :]).then_inc(consts_loaded, 16)
            sp.dma_start(bias[:, :], a["b"]).then_inc(consts_loaded, 16)
            sp.dma_start(bn1[:, 0:1], a["gamma1"]).then_inc(consts_loaded, 16)
            sp.dma_start(bn1[:, 1:2], a["beta1"]).then_inc(consts_loaded, 16)
            for k in range(TSLOTS):
                sp.dma_start(x_group[:, k, :], a["x_groups"][k * D:(k + 1) * D, :]).then_inc(x_group_loaded[k], 16)
            sp.dma_start(src_all[:, 0:tiles], a["src_cols"]).then_inc(src_loaded, 16)
            for to, of in ((to_gate, "to_gate"), (to_core, "to_core")):
                sp.dma_start(to[:, :], a[of]).then_inc(late_consts_loaded, 16)
            for to, of in ((fold, "fold"), (fold_wide, "fold_wide"), (channel_mean, "channel_mean")):
                sp.dma_start(to[:, :], a[of]).then_inc(late_consts_loaded, 16)
            for h in range(2):
                sp.dma_start(bn2[h * D:(h + 1) * D, 0:1], a["gamma2"]).then_inc(late_consts_loaded, 16)
                sp.dma_start(bn2[h * D:(h + 1) * D, 1:2], a["beta2"]).then_inc(late_consts_loaded, 16)
            with sp.Fori(1, groups // TSLOTS) as i:
                for k in range(TSLOTS):
                    sp.wait_ge(table_product, TSLOTS * (i - 1) + k + 1)
                    sp.dma_start(x_group[:, k, :], a["x_groups"][bass.ds((TSLOTS * i + k) * D, D), :])\
                        .then_inc(x_group_loaded[k], 16)
            if 2 * pairs > chunks:
                sp.wait_ge(zero_made, 1)
                sp.dma_start(z_gate[chunks * D:, :], zero[:, :]).then_inc(pad_stored, 16)
                sp.dma_start(z_core[chunks * D:, :], zero[:, :]).then_inc(pad_stored, 16)
            for k in range(TSLOTS):
                sp.wait_ge(table_stored[k], 16 * (groups // TSLOTS))
            sp.wait_ge(unfit_known, 1)

            def load_chunk(i, j, first):
                c = i * SLOTS + j
                if not first:
                    sp.wait_ge(z_done, c - SLOTS + 1)
                sp.dma_start(feats[D:P, j, :], a["edge_chunks"][bass.ds(c * D, D), :]).then_inc(edges_loaded[j], 16)
                row = sp.value_load(base_i[0:1, bass.ds(c, 1)], min_val=0, max_val=max_row)
                sp.dma_start(window[:, j, :], table[bass.ds(row, WIN), :]).then_inc(window_loaded[j], 16)

            with sp.If(flag(sp) < 1):
                for j in range(SLOTS):
                    load_chunk(0, j, True)
                with sp.Fori(1, steps) as i:
                    for j in range(SLOTS):
                        load_chunk(i, j, False)
            with sp.Else():
                with sp.Fori(0, chunks) as c:
                    sp.wait_ge(any_idx, c + 1)
                    sp.dma_start(feats[D:P, 0, :], a["edge_chunks"][bass.ds(c * D, D), :]).then_inc(any_edges, 16)
                    sp.wait_ge(any_z_copied, c + 1)
                    sp.dma_start(z_gate[bass.ds(c * D, D), :], z_out[0:D, 0, :]).then_inc(any_stored, 16)
                    sp.dma_start(z_core[bass.ds(c * D, D), :], z_out[D:P, 0, :]).then_inc(any_stored, 16)
                sp.wait_ge(any_stored, 32 * chunks)
            sp.wait_ge(late_consts_loaded, 16 * N_LATE)
            if 2 * pairs > chunks:
                sp.wait_ge(pad_stored, 32)

        @block.gpsimd
        def _(pool):
            nc.gpsimd.memset(zero[:, :], 0.0).then_inc(zero_made, 1)

            def gather(rows, idx, done):
                pool.sem_inc(gathers_due, 1)
                for t in range(TPC):
                    pool.indirect_dma_start(
                        rows[:, t * D:(t + 1) * D], None, a["x"],
                        bass.IndirectOffsetOnAxis(ap=idx[:, t:t + 1], axis=0)).then_inc(done, 16)

            def gather_chunk(i, j, at, first):
                c = i * SLOTS + j
                pool.wait_ge(idx_copied, c + 1)
                if not first:
                    pool.wait_ge(xt_done, c - AHEAD + 1)
                gather(x_src[:, at, :], src_idx[:, at, :], src_gathered[at])

            for at in range(AHEAD):
                gather_chunk(0, at, at, True)
            pool.wait_ge(unfit_known, 1)
            with pool.If(flag(pool) < 1):
                with pool.Fori(1, steps // 2) as m:
                    for at in range(AHEAD):
                        gather_chunk(2 * m, at, at, False)
                for j in range(SLOTS):
                    gather_chunk(steps - 1, j, j, False)
            with pool.Else():
                with pool.Fori(0, chunks) as c:
                    pool.wait_ge(any_idx, c + 1)
                    gather(x_src[:, 0, :], src_idx[:, 0, :], any_gathered)
                    gather(x_dst[:, :], dst_idx[:, :], any_gathered)
            pool.wait_ge(affine_step, 6)
            nc.gpsimd.tensor_tensor(small[:, 2:3], small[:, 0:1], small[:, 1:2], ALU.pow).then_inc(affine_step, 1)

        @block.vector
        def _(dve):
            done = [0]

            def step(ins):
                done[0] += 1
                ins.then_inc(window_step, 1)
                dve.wait_ge(window_step, done[0])

            def table_rest(i, k, first):
                n = TSLOTS * i + k
                dve.wait_ge(part_hi, n + 1)
                if not first:
                    dve.wait_ge(part_lo, n - TSLOTS + 1)
                nc.vector.tensor_tensor(rest[:, k, :].rearrange("p (b z) -> p b z", z=Z),
                                        product_ps[k].rearrange("p (b z) -> p b z", z=Z), parts[:, k, :, 0, :],
                                        ALU.subtract).then_inc(part_rest, 1)

            def table_lo(n, k):
                dve.wait_ge(part_mid, n + 1)
                nc.vector.tensor_tensor(parts[:, k, :, 2, :], rest[:, k, :].rearrange("p (b z) -> p b z", z=Z),
                                        parts[:, k, :, 1, :], ALU.subtract).then_inc(part_lo, 1)

            nc.vector.memset(src_all[:, tiles:], 0)
            if pair_tiles > tiles:
                nc.vector.memset(dst_f[:, tiles:], -1.0)
                nc.vector.memset(dst_local[:, tiles:], -1.0)
            step(nc.vector.memset(base_i[:, :], 0))
            dve.wait_ge(consts_loaded, 16 * N_CONSTS)
            nc.vector.tensor_copy(ident_bf[:, :], ident[:, :]).then_inc(ident_cast, 1)
            dve.wait_ge(dst_loaded, 16)
            step(nc.vector.tensor_copy(dst_f[:, 0:tiles], dst_i[:, :]))
            step(nc.vector.tensor_reduce(
                least[:, :], dst_f[:, 0:tiles].rearrange("p (c t) -> p c t", t=TPC), AX_X, ALU.min))
            table_rest(0, 0, True)
            dve.wait_ge(src_loaded, 16)
            for at in range(AHEAD):
                nc.vector.tensor_copy(src_idx[:, at, :], src_all[:, at * TPC:(at + 1) * TPC]).then_inc(idx_copied, 1)
            dve.wait_ge(least_moved, 1)
            step(nc.vector.tensor_reduce(
                least_t[0:per_group, :],
                xt_ps[0:per_group, 0:idx_groups * P].rearrange("p (g k) -> p g k", k=P), AX_X, ALU.min))
            table_rest(0, 1, True)
            table_lo(0, 0)
            dve.wait_ge(least_spread, 1)
            step(nc.vector.tensor_copy(
                base_f[:, :].rearrange("p (g k) -> p g k", k=per_group),
                dst_ps[:, 0:idx_groups * P].rearrange("p (g k) -> p g k", k=P)[:, :, 0:per_group]))
            step(nc.vector.tensor_copy(base_i[:, 0:chunks], base_f[:, :]))
            table_rest(0, 2, True)
            table_lo(1, 1)
            step(nc.vector.tensor_tensor(
                dst_local[:, 0:tiles].rearrange("p (c t) -> p c t", t=TPC),
                dst_f[:, 0:tiles].rearrange("p (c t) -> p c t", t=TPC),
                base_f[:, :].unsqueeze(2).broadcast_to([P, chunks, TPC]), ALU.subtract))
            table_rest(0, 3, True)
            table_lo(2, 2)
            step(nc.vector.tensor_reduce(top[:, :], dst_local[:, 0:tiles], AX_X, ALU.max))
            table_rest(0, 4, True)
            table_lo(3, 3)
            dve.wait_ge(top_moved, 1)
            step(nc.vector.tensor_reduce(top_one[:, 0:1], xt_ps[0:1, 0:P], AX_X, ALU.max))
            step(nc.vector.tensor_scalar(top_one[:, 1:2], top_one[:, 0:1], float(WIN), None, ALU.is_ge))
            nc.vector.tensor_copy(unfit[:, :], top_one[:, 1:2]).then_inc(unfit_known, 1)
            step(nc.vector.tensor_copy(dst_bf[:, :], dst_local[:, 0:tiles]))
            dve.wait_ge(unfit_known, 1)

            with dve.Fori(1, groups // TSLOTS) as i:
                for k in range(TSLOTS):
                    table_rest(i, k, False)
                    table_lo(TSLOTS * i + k - 1, (k - 1) % TSLOTS)
            table_lo(groups - 1, TSLOTS - 1)

            def chunk(i, j, odd, first):
                c = i * SLOTS + j
                at = odd * SLOTS + j
                dve.wait_ge(dst_spread, c + 1)
                if not first:
                    dve.wait_ge(z_done, c - SLOTS + 1)
                nc.vector.tensor_scalar(onehot_t[:, j, :], dst_ps[0:WIN, 0:CH], iota_col[0:WIN, 0:1], None,
                                        ALU.is_equal).then_inc(onehot_done, 1)
                dve.wait_ge(xt_done, c + 1)
                nc.vector.tensor_copy(src_idx[:, at, :], src_all[:, bass.ds((c + AHEAD) * TPC, TPC)])\
                    .then_inc(idx_copied, 1)
                if not (first and j == 0):
                    take_stats(c - 1, (j - 1) % SLOTS)

            def keep_moments(c, done):
                dve.wait_ge(halves_done, c + 1)
                dve.sem_inc(moments_due, 1)
                nc.vector.bn_aggr(chunk_now[:, :], stats[:, :]).then_inc(chunk_aggregated, 1)
                dve.wait_ge(chunk_aggregated, c + 1)
                nc.vector.tensor_copy(chunk_moments[:, bass.ds(c, 1), :].rearrange("p c m -> p (c m)"),
                                      chunk_now[:, :]).then_inc(done, 1)

            def take_stats(c, j):
                dve.wait_ge(z_copied, c + 1)
                for h in range(2):
                    last = nc.vector.bn_stats(stats[:, h * 6:(h + 1) * 6], z_out[:, j, h * HALF:(h + 1) * HALF])
                last.then_inc(halves_done, 1)
                keep_moments(c, stats_done)

            with dve.If(flag(dve) < 1):
                for j in range(SLOTS):
                    chunk(0, j, 0, True)
                with dve.Fori(0, steps // 2) as m:
                    for odd in (1, 0):
                        for j in range(SLOTS):
                            chunk(2 * m + 2 - odd, j, odd, False)
                take_stats(chunks - 1, SLOTS - 1)
                dve.wait_ge(stats_done, chunks)
            with dve.Else():
                dve.wait_ge(src_gathered[0], 16 * TPC)

                def any_chunk(c, first):
                    if not first:
                        dve.wait_ge(any_stats, c)
                    nc.vector.tensor_copy(src_idx[:, 0, :], src_all[:, bass.ds(c * TPC, TPC)])\
                        .then_inc(window_step, 1)
                    dve.wait_ge(window_step, done[0] + 1 + c)
                    nc.vector.tensor_copy(dst_idx[:, :], dst_i[:, bass.ds(c * TPC, TPC)]).then_inc(any_idx, 1)
                    dve.wait_ge(any_turned, c + 1)
                    nc.vector.tensor_copy(x_dst_t[:, :], dst_ps[0:D, 0:CH]).then_inc(any_dst_copied, 1)
                    dve.wait_ge(any_z_copied, c + 1)
                    for h in range(2):
                        last = nc.vector.bn_stats(stats[:, h * 6:(h + 1) * 6],
                                                  z_out[:, 0, h * HALF:(h + 1) * HALF])
                    last.then_inc(halves_done, 1)
                    keep_moments(c, any_stats)

                any_chunk(0, True)
                with dve.Fori(1, chunks) as c:
                    any_chunk(c, False)
                dve.wait_ge(any_stats, chunks)

            steps_done = [0]

            def affine_from(ins):
                steps_done[0] += 1
                ins.then_inc(affine_step, 1)
                dve.wait_ge(affine_step, steps_done[0])

            for k in range(SLOTS):
                last = nc.vector.bn_stats(mean_stats[:, 6 * k:6 * (k + 1)],
                                          chunk_moments[:, k * steps:(k + 1) * steps, 0])
            affine_from(last)
            affine_from(nc.vector.bn_aggr(moments[:, :], mean_stats[:, :]))
            affine_from(nc.vector.tensor_reduce(small[:, 0:1], chunk_moments[:, :, 1], AX_X, ALU.add))
            affine_from(nc.vector.scalar_tensor_tensor(
                out=small[:, 0:1], in0=small[:, 0:1], scalar=1.0 / chunks, in1=moments[:, 1:2],
                op0=ALU.mult, op1=ALU.add))
            affine_from(nc.vector.tensor_scalar(small[:, 0:1], small[:, 0:1], EPS, None, ALU.add))
            affine_from(nc.vector.memset(small[:, 1:2], -0.5))
            steps_done[0] += 1
            dve.wait_ge(affine_step, steps_done[0])
            affine_from(nc.vector.tensor_tensor(affine[:, 0:1], small[:, 2:3], bn1[:, 0:1], ALU.mult))
            affine_from(nc.vector.tensor_tensor(small[:, 3:4], moments[:, 0:1], affine[:, 0:1], ALU.mult))
            affine_from(nc.vector.tensor_tensor(affine[:, 1:2], bn1[:, 1:2], small[:, 3:4], ALU.subtract))
            dve.wait_ge(affine_moved, 1)
            affine_from(nc.vector.tensor_copy(gate_affine[:, :], dst_ps[:, 0:2]))
            affine_from(nc.vector.tensor_copy(core_affine[:, :], dst_ps[:, 2:4]))

        @block.tensor
        def _(pe):
            def table_group(i, k, first):
                n = TSLOTS * i + k
                pe.wait_ge(x_group_loaded[k], 16 * (i + 1))
                if not first:
                    pe.wait_ge(part_rest, n - TSLOTS + 1)
                for m in range(GROUP):
                    last = nc.tensor.matmul(product_ps[k][:, m * Z:(m + 1) * Z], x_group[:, k, m * P:(m + 1) * P],
                                            w_dst[:, :], start=True, stop=True)
                last.then_inc(table_product, 1)

            pe.wait_ge(consts_loaded, 16 * N_CONSTS)
            table_group(0, 0, True)
            table_group(0, 1, True)
            pe.wait_ge(window_step, 3)
            for k in range(idx_groups):
                last = nc.tensor.transpose(xt_ps[0:per_group, k * P:(k + 1) * P],
                                           least[:, k * per_group:(k + 1) * per_group], ident[:, :])
            last.then_inc(least_moved, 1)
            table_group(0, 2, True)
            pe.wait_ge(window_step, 4)
            for k in range(idx_groups):
                last = nc.tensor.matmul(dst_ps[:, k * P:k * P + per_group],
                                        least_t[0:per_group, k:k + 1].broadcast_to([per_group, P]),
                                        ident[0:per_group, 0:per_group], start=True, stop=True)
            last.then_inc(least_spread, 1)
            table_group(0, 3, True)
            table_group(0, 4, True)
            pe.wait_ge(window_step, 8)
            nc.tensor.transpose(xt_ps[0:1, 0:P], top[:, 0:1], ident[:, :]).then_inc(top_moved, 1)
            with pe.Fori(1, groups // TSLOTS) as i:
                for k in range(TSLOTS):
                    table_group(i, k, False)
            pe.wait_ge(part_rest, groups)
            pe.wait_ge(unfit_known, 1)
            pe.wait_ge(ident_cast, 1)
            pe.wait_ge(window_step, 11)

            def turn(to, rows):
                pe.sem_inc(turns_due, 1)
                for t in range(TPC):
                    last = nc.tensor.transpose(to[0:D, t * TILE:(t + 1) * TILE], rows[:, t * D:(t + 1) * D],
                                               ident[:, :])
                return last

            def prepare(i, j, odd, use, first):
                c = i * SLOTS + j
                if not (first and j == 0):
                    pe.wait_ge(onehot_done, c)
                for t in range(TPC):
                    last = nc.tensor.matmul(dst_ps[0:WIN, t * TILE:(t + 1) * TILE],
                                            dst_bf[:, bass.ds(c * TPC + t, 1)].broadcast_to([P, WIN]),
                                            ident_bf[:, :], start=True, stop=True)
                last.then_inc(dst_spread, 1)
                at = odd * SLOTS + j
                pe.wait_ge(src_gathered[at], 16 * TPC * use)
                if not (first and j == 0):
                    pe.wait_ge(xt_copied, c)
                turn(xt_ps, x_src[:, at, :]).then_inc(xt_done, 1)

            def form_z(i, j, first):
                c = i * SLOTS + j
                pe.wait_ge(edges_loaded[j], 16 * (i + 1))
                pe.wait_ge(window_loaded[j], 16 * (i + 1))
                pe.wait_ge(onehot_done, c + 1)
                pe.wait_ge(xt_copied, c + 1)
                if not (first and j == 0):
                    pe.wait_ge(z_copied, c)
                for h in range(2):
                    cols = slice(h * HALF, (h + 1) * HALF)
                    nc.tensor.matmul(z_halves[:, h, :], w_both[:, :], feats[:, j, cols], start=True, stop=False)
                    for part in range(PARTS):
                        last = nc.tensor.matmul(z_halves[:, h, :], window[:, j, part * Z:(part + 1) * Z],
                                                onehot_t[:, j, cols], start=False, stop=part == PARTS - 1)
                last.then_inc(z_done, 1)

            with pe.If(flag(pe) < 1):
                prepare(0, 0, 0, 1, True)
                for j in range(1, SLOTS):
                    prepare(0, j, 0, 1, True)
                    form_z(0, j - 1, True)
                with pe.Fori(0, steps // 2) as m:
                    for odd in (1, 0):
                        i = 2 * m + 2 - odd
                        for j in range(SLOTS):
                            prepare(i, j, odd, m + 2 - odd, False)
                            if j == 0:
                                form_z(i - 1, SLOTS - 1, False)
                            else:
                                form_z(i, j - 1, False)
                form_z(steps - 1, SLOTS - 1, False)
                pe.wait_ge(z_done, chunks)
            with pe.Else():
                with pe.Fori(0, chunks) as c:
                    pe.wait_ge(any_gathered, (c + 1) * 2 * TPC * 16)
                    turn(xt_ps, x_src[:, 0, :])
                    turn(dst_ps, x_dst[:, :]).then_inc(any_turned, 1)
                    pe.wait_ge(any_src_copied, c + 1)
                    pe.wait_ge(any_dst_copied, c + 1)
                    pe.wait_ge(any_edges, (c + 1) * 16)
                    for h in range(2):
                        cols = slice(h * HALF, (h + 1) * HALF)
                        nc.tensor.matmul(z_halves[:, h, :], w_both[:, :], feats[:, 0, cols], start=True, stop=False)
                        last = nc.tensor.matmul(z_halves[:, h, :], w_dst[:, :], x_dst_t[:, cols],
                                                start=False, stop=True)
                    last.then_inc(any_z, 1)
                pe.wait_ge(any_z, chunks)
            pe.wait_ge(late_consts_loaded, 16 * N_LATE)
            pe.wait_ge(affine_step, 10)
            nc.tensor.matmul(dst_ps[:, 0:2], to_gate[:, :], affine[:, :], start=True, stop=True)
            nc.tensor.matmul(dst_ps[:, 2:4], to_core[:, :], affine[:, :], start=True, stop=True)\
                .then_inc(affine_moved, 1)

        @block.scalar
        def _(act):
            def table_hi(i, k, first):
                n = TSLOTS * i + k
                act.wait_ge(table_product, n + 1)
                if not first:
                    act.wait_ge(table_stored[k], 16 * i)
                nc.scalar.activation(parts[:, k, :, 0, :], product_ps[k].rearrange("p (b z) -> p b z", z=Z),
                                     ACT.Copy).then_inc(part_hi, 1)

            def table_mid(n, k):
                act.wait_ge(part_rest, n + 1)
                nc.scalar.activation(parts[:, k, :, 1, :], rest[:, k, :].rearrange("p (b z) -> p b z", z=Z),
                                     ACT.Copy).then_inc(part_mid, 1)

            def store_table(n, k):
                act.wait_ge(part_lo, n + 1)
                act.dma_start(table[bass.ds(n * GROUP * P, GROUP * P), :].rearrange("(b p) f -> p b f", p=P),
                              parts[:, k, :, :, :].rearrange("p b s z -> p b (s z)")).then_inc(table_stored[k], 16)

            for k in range(TSLOTS):
                table_hi(0, k, True)
                if k:
                    table_mid(k - 1, k - 1)
                if k > 1:
                    store_table(k - 2, k - 2)
            with act.Fori(1, groups // TSLOTS) as i:
                for k in range(TSLOTS):
                    n = TSLOTS * i + k
                    table_hi(i, k, False)
                    table_mid(n - 1, (k - 1) % TSLOTS)
                    store_table(n - 2, (k - 2) % TSLOTS)
            table_mid(groups - 1, TSLOTS - 1)
            store_table(groups - 2, TSLOTS - 2)
            store_table(groups - 1, TSLOTS - 1)
            act.wait_ge(unfit_known, 1)
            act.wait_ge(consts_loaded, 16 * N_CONSTS)

            def copy_features(i, j, first):
                c = i * SLOTS + j
                act.wait_ge(xt_done, c + 1)
                if not first:
                    act.wait_ge(z_done, c - SLOTS + 1)
                nc.scalar.activation(feats[0:D, j, :], xt_ps[0:D, 0:CH], ACT.Copy).then_inc(xt_copied, 1)

            def copy_z(i, j, first):
                c = i * SLOTS + j
                act.wait_ge(z_done, c + 1)
                if not first:
                    act.wait_ge(z_stored[j], 32 * i)
                    act.wait_ge(stats_done, c - SLOTS + 1)
                nc.scalar.activation(z_out[:, j, :].rearrange("p (h n) -> p h n", n=HALF), z_halves,
                                     ACT.Identity, bias=bias[:, 0:1]).then_inc(z_copied, 1)
                act.wait_ge(z_copied, c + 1)
                act.dma_start(z_gate[bass.ds(c * D, D), :], z_out[0:D, j, :]).then_inc(z_stored[j], 16)
                act.dma_start(z_core[bass.ds(c * D, D), :], z_out[D:P, j, :]).then_inc(z_stored[j], 16)

            with act.If(flag(act) < 1):
                copy_features(0, 0, True)
                for j in range(1, SLOTS):
                    copy_features(0, j, True)
                    copy_z(0, j - 1, True)
                with act.Fori(1, steps) as i:
                    for j in range(SLOTS):
                        copy_features(i, j, False)
                        if j == 0:
                            copy_z(i - 1, SLOTS - 1, False)
                        else:
                            copy_z(i, j - 1, False)
                copy_z(steps - 1, SLOTS - 1, False)
                for j in range(SLOTS):
                    act.wait_ge(z_stored[j], 32 * steps)
            with act.Else():
                def any_chunk(c, first):
                    act.wait_ge(any_turned, c + 1)
                    nc.scalar.activation(feats[0:D, 0, :], xt_ps[0:D, 0:CH], ACT.Copy).then_inc(any_src_copied, 1)
                    act.wait_ge(any_z, c + 1)
                    if not first:
                        act.wait_ge(any_stored, 32 * c)
                    nc.scalar.activation(z_out[:, 0, :].rearrange("p (h n) -> p h n", n=HALF), z_halves,
                                         ACT.Identity, bias=bias[:, 0:1]).then_inc(any_z_copied, 1)

                any_chunk(0, True)
                with act.Fori(1, chunks) as c:
                    any_chunk(c, False)
                act.wait_ge(any_z_copied, chunks)


def pass2(nc, sem, sb_in, whole):
    pairs, blocks, max_row = whole.pairs, whole.blocks, whole.max_row
    z_gate, z_core = whole.z_gate, whole.z_core
    ident, iota_row, dst_f, dst_local, base_i = whole.ident, whole.iota_row, whole.dst_f, whole.dst_local, whole.base_i
    unfit, gate_affine, core_affine, sums = whole.unfit, whole.gate_affine, whole.core_affine, whole.sums
    body = 2 * PPH
    loops = pairs // body
    left = pairs - loops * body
    assert loops >= 3 and left <= PPH
    ptiles = 2 * TPC
    RING = 3
    HOTS = 4

    ctx = ExitStack()
    with ctx:
        def sb(name, shape, dt=F32):
            return sb_in(ctx, name, shape, dt)

        def ps(name, shape):
            return ctx.enter_context(nc.psum_tensor(name, shape, F32))

        gate = sb("gate", [P, 2, PPH * CH])
        core = sb("core", [P, 2, PPH * CH])
        soft = sb("soft", [P, 2, PPH * CH])
        message = sb("message", [P, RING, CH])
        onehot = sb("onehot", [P, HOTS, ptiles, WIN])
        any_hot = onehot[:, :, :, :].rearrange("p u t w -> p (u t w)")[:, 0:TPC * P]\
            .rearrange("p (t w) -> p t w", w=P)
        any_local = sb("any_local", [P, TPC])
        turn_ps = ps("turn_ps", [P, RING, 2 * BANK])
        sum_ps = ps("sum_ps", [P, 2, BANK])

        sums_zero = sem("sums_zero")
        gate_loaded = [[sem(f"gate_loaded{s}_{q}") for q in range(PPH // PIECE)] for s in range(2)]
        core_loaded = [[sem(f"core_loaded{s}_{q}") for q in range(PPH // PIECE)] for s in range(2)]
        sigmoid_done = sem("sigmoid_done")
        norms_due = sem("norms_due")
        normed = sem("normed")
        capped = sem("capped")
        exp_done = sem("exp_done")
        log_done = sem("log_done")
        softplus_done = sem("softplus_done")
        product_done = sem("product_done")
        turned = sem("turned")
        message_copied = sem("message_copied")
        onehot_made = sem("onehot_made")
        summed = sem("summed")
        sums_added = sem("sums_added")
        any_pair = sem("any_pair")
        any_local_made = sem("any_local_made")
        any_onehot = sem("any_onehot")
        any_summed = sem("any_summed")
        any_added = sem("any_added")

        def pieces(n):
            return [(q, min(PIECE, n - q * PIECE)) for q in range(-(-n // PIECE))]

        def spans(n):
            return [(lo, min(hi, n)) for lo, hi in ((0, 2 * PIECE), (2 * PIECE, PPH)) if lo < n]

        def place(i, k):
            return 2 * i + k // PPH, k % PPH

        block = ctx.enter_context(nc.Block())

        def flag(eng):
            return eng.value_load(unfit[0:1, 0:1], min_val=0, max_val=1)

        @block.sync
        def _(sp):
            def load_half(i, s, n, first):
                half = 2 * i + s
                for q, m in pieces(n):
                    for buf, z, loaded, used in ((core, z_core, core_loaded, softplus_done),
                                                 (gate, z_gate, gate_loaded, product_done)):
                        if not first:
                            sp.wait_ge(used, (half - 2) * PPH + (q + 1) * PIECE)
                        sp.dma_start(buf[:, s, q * PIECE * CH:(q * PIECE + m) * CH].rearrange("p (k n) -> p k n", n=CH),
                                     z[bass.ds((half * PPH + q * PIECE) * P, m * P), :]
                                     .rearrange("(k p) n -> p k n", p=P)).then_inc(loaded[s][q], 16)

            with sp.If(flag(sp) < 1):
                for s in range(2):
                    load_half(0, s, PPH, True)
                with sp.Fori(1, loops) as i:
                    for s in range(2):
                        load_half(i, s, PPH, False)
                if left:
                    load_half(loops, 0, left, False)
                sp.wait_ge(product_done, pairs)
            with sp.Else():
                def any_load(u, first):
                    if not first:
                        sp.wait_ge(any_pair, u)
                    sp.dma_start(gate[:, 0, 0:CH], z_gate[bass.ds(u * P, P), :]).then_inc(gate_loaded[0][0], 16)
                    sp.dma_start(core[:, 0, 0:CH], z_core[bass.ds(u * P, P), :]).then_inc(core_loaded[0][0], 16)

                any_load(0, True)
                with sp.Fori(1, pairs) as u:
                    any_load(u, False)
                sp.wait_ge(any_pair, pairs)

        @block.gpsimd
        def _(pool):
            def norm(s, first_pair, n):
                cols = slice(first_pair * CH, (first_pair + n) * CH)
                pool.sem_inc(norms_due, 1)
                nc.gpsimd.tensor_scalar(core[:, s, cols], core[:, s, cols], core_affine[:, 0:1],
                                        core_affine[:, 1:2], ALU.mult, ALU.add).then_inc(normed, 1)

            def cap(s, first_pair, n, number):
                cols = slice(first_pair * CH, (first_pair + n) * CH)
                pool.wait_ge(normed, number + 1)
                pool.sem_inc(norms_due, 1)
                nc.gpsimd.tensor_scalar(soft[:, s, cols], core[:, s, cols], SP_CAP, None, ALU.min)\
                    .then_inc(capped, 1)

            def norm_half(i, s, n, first):
                half = 2 * i + s
                for q, m in pieces(n):
                    pool.wait_ge(core_loaded[s][q], 16 * (i + 1))
                    norm(s, q * PIECE, m)
                    if not first:
                        pool.wait_ge(turned, (half - 2) * PPH + (q + 1) * PIECE)
                    cap(s, q * PIECE, m, half * (PPH // PIECE) + q)

            with pool.If(flag(pool) < 1):
                for s in range(2):
                    norm_half(0, s, PPH, True)
                with pool.Fori(1, loops) as i:
                    for s in range(2):
                        norm_half(i, s, PPH, False)
                if left:
                    norm_half(loops, 0, left, False)
            with pool.Else():
                with pool.Fori(0, pairs) as u:
                    pool.wait_ge(core_loaded[0][0], 16 * (u + 1))
                    norm(0, 0, 1)
                    cap(0, 0, 1, u)
            pool.wait_ge(sums_zero, 1)

        @block.scalar
        def _(act):
            def gates(s, lo, hi):
                cols = slice(lo * CH, hi * CH)
                nc.scalar.activation(gate[:, s, cols], gate[:, s, cols], ACT.Sigmoid,
                                     bias=gate_affine[:, 1:2], scale=gate_affine[:, 0:1]).then_inc(sigmoid_done, 1)

            def exps(s, lo, hi):
                cols = slice(lo * CH, hi * CH)
                nc.scalar.activation(soft[:, s, cols], soft[:, s, cols], ACT.Exp).then_inc(exp_done, 1)

            def logs(s, lo, hi, number):
                cols = slice(lo * CH, hi * CH)
                act.wait_ge(exp_done, number + 1)
                nc.scalar.activation(soft[:, s, cols], soft[:, s, cols], ACT.Ln, bias=1.0).then_inc(log_done, 1)

            def copy_message(i, k, first):
                u = i * body + k
                act.wait_ge(turned, u + 1)
                if not first:
                    act.wait_ge(summed, u - RING + 1)
                nc.scalar.activation(message[:, k % RING, :], turn_ps[:, k % RING, 0:CH], ACT.Copy)\
                    .then_inc(message_copied, 1)

            COPY_LAG = 4

            def body_steps(i, n_a, n_b, n_next, first=False):
                ready = iter(range(0 if first else -COPY_LAG, body - COPY_LAG if n_next else n_a + n_b))

                def copy_one():
                    for k in ready:
                        copy_message(i, k, first and k < RING)
                        break

                def copy_behind(s):
                    if not first or s:
                        copy_one()

                def softplus_half(s, n):
                    number = 2 * i + s
                    for lo, hi in spans(n):
                        act.wait_ge(capped, number * (PPH // PIECE) + -(-hi // PIECE))
                        exps(s, lo, hi)
                        copy_behind(s)
                    for at, (lo, hi) in enumerate(spans(n)):
                        logs(s, lo, hi, 2 * number + at)
                        copy_behind(s)

                nc.scalar.preload_act_table_set(EXP_LN_SET)
                softplus_half(0, n_a)
                if n_b:
                    softplus_half(1, n_b)
                    gate_half(1, i, n_b, copy_one)
                if n_next:
                    gate_half(0, i + 1, n_next, copy_one)
                for k in ready:
                    copy_message(i, k, first and k < RING)

            def gate_half(s, run, n, copy_one):
                for lo, hi in spans(n):
                    for q in range(lo // PIECE, -(-hi // PIECE)):
                        act.wait_ge(gate_loaded[s][q], 16 * (run + 1))
                    gates(s, lo, hi)
                    copy_one()

            with act.If(flag(act) < 1):
                gate_half(0, 0, PPH, lambda: None)
                body_steps(0, PPH, PPH, PPH, first=True)
                with act.Fori(1, loops - 1) as i:
                    body_steps(i, PPH, PPH, PPH)
                if left:
                    body_steps(loops - 1, PPH, PPH, left)
                    body_steps(loops, left, 0, 0)
                else:
                    body_steps(loops - 1, PPH, PPH, 0)
                act.wait_ge(log_done, 4 * loops + len(spans(left)))
            with act.Else():
                with act.Fori(0, pairs) as u:
                    act.wait_ge(gate_loaded[0][0], 16 * (u + 1))
                    gates(0, 0, 1)
                    nc.scalar.preload_act_table_set(EXP_LN_SET)
                    act.wait_ge(capped, u + 1)
                    exps(0, 0, 1)
                    logs(0, 0, 1, u)
                act.wait_ge(log_done, pairs)

        @block.vector
        def _(dve):
            nc.vector.memset(sums[:, :], 0.0).then_inc(sums_zero, 1)
            dve.wait_ge(sums_zero, 1)

            iota_many = iota_row[:, 0:WIN].unsqueeze(1).broadcast_to([P, ptiles, WIN])

            def mark(u, k, first):
                if not first:
                    dve.wait_ge(summed, u - HOTS + 1)
                nc.vector.tensor_tensor(
                    onehot[:, k % HOTS, :, :], iota_many,
                    dst_local[:, bass.ds(u * ptiles, ptiles)].unsqueeze(2).broadcast_to([P, ptiles, WIN]),
                    ALU.is_equal).then_inc(onehot_made, 1)

            def softplus(s, p, span):
                cols = slice(p * CH, (p + 1) * CH)
                dve.wait_ge(log_done, span + 1)
                nc.vector.tensor_tensor(soft[:, s, cols], soft[:, s, cols], core[:, s, cols], ALU.max)\
                    .then_inc(softplus_done, 1)

            def product(s, p, u, span):
                cols = slice(p * CH, (p + 1) * CH)
                dve.wait_ge(softplus_done, u + 1)
                dve.wait_ge(sigmoid_done, span + 1)
                nc.vector.tensor_tensor(soft[:, s, cols], soft[:, s, cols], gate[:, s, cols], ALU.mult)\
                    .then_inc(product_done, 1)

            def window_starts(u):
                return [dve.value_load(base_i[0:1, bass.ds(2 * u + h, 1)], min_val=0, max_val=max_row)
                        for h in range(2)]

            def add_sums(u, r, starts, first):
                dve.wait_ge(summed, u + 1)
                for h, node in enumerate(starts):
                    rows = slice(h * D, (h + 1) * D)
                    if not first:
                        dve.wait_ge(sums_added, 2 * u + h - 1)
                    nc.vector.tensor_tensor(sums[rows, bass.ds(node, WIN)], sums[rows, bass.ds(node, WIN)],
                                            sum_ps[rows, r, 0:WIN], ALU.add).then_inc(sums_added, 1)

            def pair(i, k, first):
                u = i * body + k
                half, p = place(i, k)
                span = 2 * half + p // (2 * PIECE)
                softplus(k // PPH, p, span)
                starts = None if first and k < 3 else window_starts(u - 3)
                mark(u, k, first and k < HOTS)
                product(k // PPH, p, u, span)
                if starts:
                    add_sums(u - 3, (k - 3) % 2, starts, first and k == 3)

            with dve.If(flag(dve) < 1):
                for k in range(body):
                    pair(0, k, True)
                with dve.Fori(1, loops) as i:
                    for k in range(body):
                        pair(i, k, False)
                for k in range(left):
                    pair(loops, k, False)
                for u in range(pairs - 3, pairs):
                    add_sums(u, u % 2, window_starts(u), False)
                dve.wait_ge(sums_added, 2 * pairs)
            with dve.Else():
                def any_window(u, h, w):
                    n = (2 * u + h) * blocks + w
                    rows = slice(h * D, (h + 1) * D)
                    dve.wait_ge(any_local_made, n + 2 * u + h + 1)
                    nc.vector.tensor_tensor(
                        any_hot, iota_row[:, :].unsqueeze(1).broadcast_to([P, TPC, P]),
                        any_local[:, :].unsqueeze(2).broadcast_to([P, TPC, P]), ALU.is_equal)\
                        .then_inc(any_onehot, 1)
                    dve.wait_ge(any_onehot, n + 1)
                    nc.vector.tensor_scalar(any_local[:, :], any_local[:, :], float(P), None, ALU.subtract)\
                        .then_inc(any_local_made, 1)
                    dve.wait_ge(any_summed, n + 1)
                    nc.vector.tensor_tensor(sums[rows, bass.ds(w * P, P)], sums[rows, bass.ds(w * P, P)],
                                            sum_ps[rows, 0, 0:P], ALU.add).then_inc(any_added, 1)

                with dve.Fori(0, pairs) as u:
                    softplus(0, 0, u)
                    product(0, 0, u, u)
                    dve.wait_ge(turned, u + 1)
                    nc.vector.tensor_copy(message[:, 0, :], turn_ps[:, 0, 0:CH]).then_inc(message_copied, 1)
                    for h in range(2):
                        if h:
                            dve.wait_ge(any_local_made, (2 * u + h) * (blocks + 1))
                        nc.vector.tensor_copy(any_local[:, :], dst_f[:, bass.ds((2 * u + h) * TPC, TPC)])\
                            .then_inc(any_local_made, 1)
                        with dve.Fori(0, blocks) as w:
                            any_window(u, h, w)
                    dve.wait_ge(any_local_made, (2 * u + 2) * (blocks + 1))
                    dve.wait_ge(any_added, (2 * u + 2) * blocks)
                    nc.vector.memset(any_local[:, :], 0.0).then_inc(any_pair, 1)
                    dve.wait_ge(any_pair, u + 1)

        @block.tensor
        def _(pe):
            def turn(s, p, r):
                for t in range(TPC):
                    at = p * CH + t * TILE
                    last = nc.tensor.transpose(turn_ps[:, r, t * P:(t + 1) * P], soft[:, s, at:at + TILE],
                                               ident[:, :])
                last.then_inc(turned, 1)

            def turn_pair(i, k, first):
                pe.wait_ge(product_done, i * body + k + 1)
                if not first:
                    pe.wait_ge(message_copied, i * body + k - RING + 1)
                turn(k // PPH, k % PPH, k % RING)

            def sum_pair(i, k, first):
                u = i * body + k
                pe.wait_ge(message_copied, u + 1)
                pe.wait_ge(onehot_made, u + 1)
                if not first:
                    pe.wait_ge(sums_added, 2 * u - 2)
                for h in range(2):
                    for t in range(TPC):
                        last = nc.tensor.matmul(sum_ps[h * D:(h + 1) * D, k % 2, 0:WIN],
                                                message[:, k % RING, t * P + h * D:t * P + (h + 1) * D],
                                                onehot[:, k % HOTS, h * TPC + t, :],
                                                start=t == 0, stop=t == TPC - 1)
                last.then_inc(summed, 1)

            def pair(i, k, first):
                if not (first and k < 2):
                    sum_pair(i, k - 2, first and k < 4)
                turn_pair(i, k, first and k < RING)

            with pe.If(flag(pe) < 1):
                for k in range(body):
                    pair(0, k, True)
                with pe.Fori(1, loops) as i:
                    for k in range(body):
                        pair(i, k, False)
                for k in range(left):
                    pair(loops, k, False)
                for k in range(left - 2, left):
                    sum_pair(loops, k, False)
                pe.wait_ge(summed, pairs)
            with pe.Else():
                with pe.Fori(0, pairs) as u:
                    pe.wait_ge(product_done, u + 1)
                    turn(0, 0, 0)
                    for h in range(2):
                        with pe.Fori(0, blocks) as w:
                            pe.wait_ge(message_copied, u + 1)
                            pe.wait_ge(any_onehot, (2 * u + h) * blocks + w + 1)
                            for t in range(TPC):
                                last = nc.tensor.matmul(sum_ps[h * D:(h + 1) * D, 0, 0:P],
                                                        message[:, 0, t * P + h * D:t * P + (h + 1) * D],
                                                        any_hot[:, t, :],
                                                        start=t == 0, stop=t == TPC - 1)
                            last.then_inc(any_summed, 1)
                pe.wait_ge(any_summed, 2 * pairs * blocks)


def nodes(nc, a, out, sem, sb_in, whole):
    n_nodes = a["x"].shape[0]
    half = n_nodes // 2
    sums, fold, fold_wide, channel_mean, bn2 = whole.sums, whole.fold, whole.fold_wide, whole.channel_mean, whole.bn2
    pieces = [(at, min(BANK, half - at)) for at in range(0, half, BANK)]
    n = len(pieces)

    ctx = ExitStack()
    with ctx:
        def sb(name, shape, dt=F32):
            return sb_in(ctx, name, shape, dt)

        def ps(name, shape):
            return ctx.enter_context(nc.psum_tensor(name, shape, F32))

        x_half = sb("x_half", [P, half])
        update = sb("update", [P, half])
        work = sb("work", [P, half])
        total = sb("total", [P, half])
        stats2 = sb("stats2", [P, 6 * n])
        moments2 = sb("moments2", [P, 2])
        small2 = sb("small2", [P, 6])
        eps_col = sb("eps_col", [P, 1])
        node_ps = ps("node_ps", [P, 2, BANK])
        mean_ps = ps("mean_ps", [P, 2, BANK])
        var_ps = ps("var_ps", [P, 2, BANK])
        both_ps = ps("both_ps", [P, BANK])

        x_loaded = sem("x_loaded")
        eps_set = sem("eps_set")
        folded = sem("folded")
        fold_copied = sem("fold_copied")
        stats2_step = sem("stats2_step")
        both_added = sem("both_added")
        power_done = sem("power_done")
        offset_step = sem("offset_step")
        scaled = sem("scaled")
        capped = sem("node_capped")
        exp_done = sem("node_exp_done")
        log_done = sem("node_log_done")
        softplus_done = sem("node_softplus_done")
        total_done = sem("total_done")
        mean_done = sem("mean_done")
        centered = sem("centered")
        squared = sem("squared")
        var_done = sem("var_done")
        var_log = sem("var_log")
        deviation_done = sem("deviation_done")
        result_done = sem("result_done")
        out_stored = sem("out_stored")
        block = ctx.enter_context(nc.Block())

        def cols(k):
            at, width = pieces[k]
            return slice(at, at + width)

        def width(k):
            return slice(0, pieces[k][1])

        @block.sync
        def _(sp):
            sp.dma_start(x_half[:, :], a["x_halves"]).then_inc(x_loaded, 16)
            for k in range(n):
                sp.wait_ge(result_done, k + 1)
                sp.dma_start(out[:, cols(k)], total[:, cols(k)]).then_inc(out_stored, 16)
            sp.wait_ge(out_stored, 16 * n)

        @block.gpsimd
        def _(pool):
            pool.wait_ge(stats2_step, n + 8)
            nc.gpsimd.tensor_tensor(small2[:, 4:5], small2[:, 2:3], small2[:, 3:4], ALU.pow).then_inc(power_done, 1)
            for k in range(n):
                pool.wait_ge(softplus_done, k + 1)
                nc.gpsimd.tensor_tensor(total[:, cols(k)], work[:, cols(k)], x_half[:, cols(k)], ALU.add)\
                    .then_inc(total_done, 1)

        @block.scalar
        def _(act):
            for k in range(n):
                act.wait_ge(folded, k + 1)
                nc.scalar.activation(update[:, cols(k)], node_ps[:, k % 2, width(k)], ACT.Copy).then_inc(fold_copied, 1)
            nc.scalar.preload_act_table_set(EXP_LN_SET)
            act.wait_ge(eps_set, 1)

            def softplus(k):
                act.wait_ge(capped, k + 1)
                nc.scalar.activation(work[:, cols(k)], work[:, cols(k)], ACT.Exp).then_inc(exp_done, 1)
                act.wait_ge(exp_done, k + 1)
                nc.scalar.activation(work[:, cols(k)], work[:, cols(k)], ACT.Ln, bias=1.0).then_inc(log_done, 1)

            def square(k):
                act.wait_ge(centered, k + 1)
                nc.scalar.activation(work[:, cols(k)], total[:, cols(k)], ACT.Square).then_inc(squared, 1)

            def deviation(k):
                act.wait_ge(var_done, k + 1)
                nc.scalar.activation(work[:, cols(k)], var_ps[:, k % 2, width(k)], ACT.Ln,
                                     bias=eps_col[:, 0:1]).then_inc(var_log, 1)
                act.wait_ge(var_log, k + 1)
                nc.scalar.activation(work[:, cols(k)], work[:, cols(k)], ACT.Exp, scale=-0.5)\
                    .then_inc(deviation_done, 1)

            for k in range(n + 4):
                if k < n:
                    softplus(k)
                if 2 <= k < n + 2:
                    square(k - 2)
                if 4 <= k:
                    deviation(k - 4)

        @block.tensor
        def _(pe):
            for k in range(n):
                if k >= 2:
                    pe.wait_ge(fold_copied, k - 1)
                for h in range(2):
                    at, size = pieces[k]
                    last = nc.tensor.matmul(node_ps[h * D:(h + 1) * D, k % 2, 0:size], fold[:, :],
                                            sums[:, h * half + at:h * half + at + size], start=True, stop=True)
                last.then_inc(folded, 1)
            pe.wait_ge(stats2_step, n + 1)
            nc.tensor.matmul(both_ps[:, 0:2], fold_wide[:, :], moments2[:, :], start=True, stop=True)\
                .then_inc(both_added, 1)
            for k in range(n + 1):
                if k < n:
                    pe.wait_ge(total_done, k + 1)
                    if k >= 2:
                        pe.wait_ge(centered, k - 1)
                    nc.tensor.matmul(mean_ps[:, k % 2, width(k)], channel_mean[:, :], total[:, cols(k)],
                                     start=True, stop=True).then_inc(mean_done, 1)
                if k >= 1:
                    pe.wait_ge(squared, k)
                    if k >= 3:
                        pe.wait_ge(var_log, k - 2)
                    nc.tensor.matmul(var_ps[:, (k - 1) % 2, width(k - 1)], channel_mean[:, :],
                                     work[:, cols(k - 1)], start=True, stop=True).then_inc(var_done, 1)

        @block.vector
        def _(dve):
            nc.vector.memset(eps_col[:, :], EPS).then_inc(eps_set, 1)
            for k in range(n):
                dve.wait_ge(fold_copied, k + 1)
                nc.vector.bn_stats(stats2[:, 6 * k:6 * (k + 1)], update[:, cols(k)]).then_inc(stats2_step, 1)
            done = [n]

            def step(ins):
                done[0] += 1
                ins.then_inc(stats2_step, 1)
                dve.wait_ge(stats2_step, done[0])

            dve.wait_ge(stats2_step, n)
            step(nc.vector.bn_aggr(moments2[:, :], stats2[:, :]))
            dve.wait_ge(both_added, 1)
            step(nc.vector.tensor_scalar(small2[:, 0:2], both_ps[:, 0:2], 0.5, None, ALU.mult))
            step(nc.vector.tensor_tensor(small2[:, 2:3], moments2[:, 0:1], small2[:, 0:1], ALU.subtract))
            step(nc.vector.tensor_tensor(small2[:, 2:3], small2[:, 2:3], small2[:, 2:3], ALU.mult))
            step(nc.vector.tensor_tensor(small2[:, 2:3], small2[:, 2:3], small2[:, 1:2], ALU.add))
            step(nc.vector.tensor_scalar(small2[:, 2:3], small2[:, 2:3], EPS, None, ALU.add))
            step(nc.vector.memset(small2[:, 3:4], -0.5))
            step(nc.vector.tensor_copy(small2[:, 5:6], bn2[:, 1:2]))
            dve.wait_ge(power_done, 1)
            step(nc.vector.tensor_tensor(small2[:, 4:5], small2[:, 4:5], bn2[:, 0:1], ALU.mult))
            step(nc.vector.tensor_tensor(small2[:, 3:4], small2[:, 0:1], small2[:, 4:5], ALU.mult))
            step(nc.vector.tensor_tensor(small2[:, 5:6], small2[:, 5:6], small2[:, 3:4], ALU.subtract))
            scale, offset = small2[:, 4:5], small2[:, 5:6]
            dve.wait_ge(x_loaded, 16)

            def node_update(k):
                nc.vector.scalar_tensor_tensor(out=update[:, cols(k)], in0=update[:, cols(k)], scalar=scale,
                                               in1=x_half[:, cols(k)], op0=ALU.mult, op1=ALU.add).then_inc(scaled, 1)
                dve.wait_ge(scaled, k + 1)
                nc.vector.tensor_scalar(work[:, cols(k)], update[:, cols(k)], offset, SP_CAP, ALU.add, ALU.min)\
                    .then_inc(capped, 1)

            def softplus(k):
                dve.wait_ge(log_done, k + 1)
                nc.vector.scalar_tensor_tensor(out=work[:, cols(k)], in0=update[:, cols(k)], scalar=offset,
                                               in1=work[:, cols(k)], op0=ALU.add, op1=ALU.max)\
                    .then_inc(softplus_done, 1)

            def center(k):
                dve.wait_ge(mean_done, k + 1)
                nc.vector.tensor_tensor(total[:, cols(k)], total[:, cols(k)], mean_ps[:, k % 2, width(k)],
                                        ALU.subtract).then_inc(centered, 1)

            def result(k):
                dve.wait_ge(deviation_done, k + 1)
                nc.vector.tensor_tensor(total[:, cols(k)], total[:, cols(k)], work[:, cols(k)], ALU.mult)\
                    .then_inc(result_done, 1)

            for k in range(n + 5):
                if k < n:
                    node_update(k)
                if 1 <= k < n + 1:
                    softplus(k - 1)
                if 2 <= k < n + 2:
                    center(k - 2)
                if 5 <= k:
                    result(k - 5)
            dve.wait_ge(result_done, n)


def kernel(**inputs):
    import concourse.bacc as bacc
    from concourse.bass_utils import run_bass_kernel_spmd

    x = np.asarray(inputs["x"])
    src = np.asarray(inputs["src"])
    dst = np.asarray(inputs["dst"])
    edges = np.asarray(inputs["edge_attr_64"])
    n_nodes, n_edges = x.shape[0], src.shape[0]
    chunks, blocks, groups, pairs = sizes(n_nodes, n_edges)

    x_t = np.zeros((D, groups * GROUP * P), x.dtype)
    x_t[:, :n_nodes] = x.T
    iota = np.arange(P, dtype=np.float32)
    arrays = {
        "x": x,
        "x_groups": np.ascontiguousarray(x_t.reshape(D, groups, GROUP * P).transpose(1, 0, 2)).reshape(-1, GROUP * P),
        "src_cols": np.ascontiguousarray(src.reshape(-1, TILE).T),
        "dst_cols": np.ascontiguousarray(dst.reshape(-1, TILE).T),
        "edge_chunks": np.ascontiguousarray(edges.reshape(chunks, CH, D).transpose(0, 2, 1)).reshape(-1, CH),
        "w": np.asarray(inputs["L0_gnn_W"]),
        "b": np.asarray(inputs["L0_gnn_b"]).reshape(Z, 1),
        "gamma1": np.asarray(inputs["L0_gnn_bn1_gamma"]).reshape(Z, 1),
        "beta1": np.asarray(inputs["L0_gnn_bn1_beta"]).reshape(Z, 1),
        "gamma2": np.asarray(inputs["L0_gnn_bn2_gamma"]).reshape(D, 1),
        "beta2": np.asarray(inputs["L0_gnn_bn2_beta"]).reshape(D, 1),
        "ident": np.eye(P, dtype=np.float32),
        "iota_row": np.tile(iota, (P, 1)),
        "iota_col": iota.reshape(P, 1).copy(),
        "to_gate": np.vstack([np.tile(np.eye(D, dtype=np.float32), (1, 2)), np.zeros((D, P), np.float32)]),
        "to_core": np.vstack([np.zeros((D, P), np.float32), np.tile(np.eye(D, dtype=np.float32), (1, 2))]),
        "fold": np.tile(np.eye(D, dtype=np.float32), (2, 1)),
        "fold_wide": np.tile(np.eye(D, dtype=np.float32), (2, 2)),
        "channel_mean": np.kron(np.eye(2, dtype=np.float32), np.full((D, D), 1.0 / D, np.float32)),
        "x_halves": np.ascontiguousarray(x.reshape(2, n_nodes // 2, D).transpose(0, 2, 1)).reshape(P, -1),
    }
    nc = bacc.Bacc("TRN2", target_bir_lowering=False, num_devices=1)
    aps = {name: nc.dram_tensor(f"in_{name}", v.shape, mybir.dt.from_np(v.dtype), kind="ExternalInput").ap()
           for name, v in arrays.items()}
    out = nc.dram_tensor("out", (P, n_nodes // 2), F32, kind="ExternalOutput").ap()
    build_program(nc, aps, out)
    got = run_bass_kernel_spmd(nc, [{f"in_{name}": v for name, v in arrays.items()}], core_ids=[0])
    return np.asarray(got.results[0]["out"]).reshape(2, D, n_nodes // 2).transpose(0, 2, 1).reshape(n_nodes, D)
```
